# Optimizing a Trainium2 kernel written in Bass

```python
import numpy as np
import jax
import jax.numpy as jnp

def _softmax(x, axis=-1):
    return jax.nn.softmax(x, axis=axis)

def _gelu(x):
    return jax.nn.gelu(x, approximate=True)

def _silu(x):
    return jax.nn.silu(x)

def _sigmoid(x):
    return jax.nn.sigmoid(x)

def _layernorm(x, axis=-1, eps=1e-05):
    m = jnp.mean(x, axis=axis, keepdims=True)
    v = jnp.var(x, axis=axis, keepdims=True)
    return (x - m) / jnp.sqrt(v + eps)

def _scatter_add(tgt, idx, src, axis=0):
    return tgt.at[idx].add(src)

def _segment_sum(src, seg, n):
    return jax.ops.segment_sum(src, seg, n)
kernel_name = 'mk_sandwich_d1_jaxref_r4_c40fd2'

def setup_inputs(seed: int=0):
    np.random.seed(seed)
    _w = jnp.asarray

    def _L0_attn_setup():
        import jax, jax.numpy as jnp
        import numpy as np
        D, E, N, D_DELTA, D_CONV = (512, 1024, 16, 128, 4)
        B_SZ, L = (1, 512)
        EPS = 1e-05

        def _silu(x):
            return x * jax.nn.sigmoid(x)
        key = jax.random.key(seed)
        ks = jax.random.split(key, 16)
        s = lambda k, shape, scale: jax.random.normal(k, shape, dtype=jnp.float32) * scale
        return {'resid': s(ks[0], (B_SZ, L, D), 1.0), 'norm_w': jnp.ones((D,), jnp.float32), 'W_skip': s(ks[1], (D, E), D ** (-0.5)), 'W_in': s(ks[2], (D, E), D ** (-0.5)), 'conv_w': s(ks[3], (D_CONV, 1, E), D_CONV ** (-0.5)), 'conv_b': s(ks[4], (E,), 0.02), 'W_delta_1': s(ks[5], (E, D_DELTA), E ** (-0.5)), 'W_delta_2': s(ks[6], (D_DELTA, E), D_DELTA ** (-0.5)), 'b_delta_2': s(ks[7], (E,), 0.02), 'W_B': s(ks[8], (E, N), E ** (-0.5)), 'W_C': s(ks[9], (E, N), E ** (-0.5)), 'A_log': s(ks[10], (E, N), 0.5), 'W_D': jnp.ones((E,), jnp.float32), 'W_out': s(ks[11], (E, D), E ** (-0.5))}
    _L0_attn_in = _L0_attn_setup()

    def _L0_ffn_setup():
        import jax, jax.numpy as jnp
        import numpy as np
        TOP_K = 8
        key = jax.random.key(seed)
        k1, k2, k3 = jax.random.split(key, 3)
        B, S, H, E = (4, 1024, 512, 64)
        hidden_states = jax.random.normal(k1, (B, S, H), dtype=jnp.float32)
        router_weight = jax.random.normal(k2, (E, H), dtype=jnp.float32)
        router_bias = jnp.zeros((E,), dtype=jnp.float32)
        expert_bias = jax.random.normal(k3, (E, H), dtype=jnp.float32) * 0.1
        return {'hidden_states': hidden_states, 'router_weight': router_weight, 'router_bias': router_bias, 'expert_bias': expert_bias}
    _L0_ffn_in = _L0_ffn_setup()
    _d = {'L0_attn_resid': _L0_attn_in['resid'], 'L0_attn_norm_w': _L0_attn_in['norm_w'], 'L0_attn_W_skip': _L0_attn_in['W_skip'], 'L0_attn_W_in': _L0_attn_in['W_in'], 'L0_attn_conv_w': _L0_attn_in['conv_w'], 'L0_attn_conv_b': _L0_attn_in['conv_b'], 'L0_attn_W_delta_1': _L0_attn_in['W_delta_1'], 'L0_attn_W_delta_2': _L0_attn_in['W_delta_2'], 'L0_attn_b_delta_2': _L0_attn_in['b_delta_2'], 'L0_attn_W_B': _L0_attn_in['W_B'], 'L0_attn_W_C': _L0_attn_in['W_C'], 'L0_attn_A_log': _L0_attn_in['A_log'], 'L0_attn_W_D': _L0_attn_in['W_D'], 'L0_attn_W_out': _L0_attn_in['W_out'], 'L0_ffn_router_weight': _L0_ffn_in['router_weight'], 'L0_ffn_router_bias': _L0_ffn_in['router_bias'], 'L0_ffn_expert_bias': _L0_ffn_in['expert_bias']}
    _x0 = _d['L0_attn_resid']
    _d['L0_attn_resid'] = jax.random.normal(jax.random.fold_in(jax.random.key(seed), 1), (2, 2048, 512), dtype=_x0.dtype)
    del _x0
    return _d

def reference(L0_attn_resid, L0_attn_norm_w, L0_attn_W_skip, L0_attn_W_in, L0_attn_conv_w, L0_attn_conv_b, L0_attn_W_delta_1, L0_attn_W_delta_2, L0_attn_b_delta_2, L0_attn_W_B, L0_attn_W_C, L0_attn_A_log, L0_attn_W_D, L0_attn_W_out, L0_ffn_router_weight, L0_ffn_router_bias, L0_ffn_expert_bias):

    def _L0_attn_ref(resid, norm_w, W_skip, W_in, conv_w, conv_b, W_delta_1, W_delta_2, b_delta_2, W_B, W_C, A_log, W_D, W_out):
        import jax, jax.numpy as jnp
        import numpy as np
        D, E, N, D_DELTA, D_CONV = (512, 1024, 16, 128, 4)
        B_SZ, L = (1, 512)
        EPS = 1e-05

        def _silu(x):
            return x * jax.nn.sigmoid(x)
        resid_norm = resid * jax.lax.rsqrt(jnp.mean(resid * resid, axis=-1, keepdims=True) + EPS) * norm_w
        skip = resid_norm @ W_skip
        x_in = resid_norm @ W_in
        conv = jax.lax.conv_general_dilated(x_in, conv_w, window_strides=(1,), padding=[(D_CONV - 1, 0)], dimension_numbers=('NWC', 'WIO', 'NWC'), feature_group_count=E)
        x = _silu(conv + conv_b)
        delta = jax.nn.softplus(x @ W_delta_1 @ W_delta_2 + b_delta_2)
        Bm = x @ W_B
        Cm = x @ W_C
        A = -jnp.exp(A_log)

        def step(h, inp):
            d_l, B_l, C_l, x_l = inp
            A_bar = jnp.exp(d_l[:, :, None] * A)
            h = h * A_bar + (d_l * x_l)[:, :, None] * B_l[:, None, :]
            y_l = jnp.einsum('ben,bn->be', h, C_l)
            return (h, y_l)
        h0 = jnp.zeros((resid.shape[0], E, N), x.dtype)
        xs = (jnp.swapaxes(delta, 0, 1), jnp.swapaxes(Bm, 0, 1), jnp.swapaxes(Cm, 0, 1), jnp.swapaxes(x, 0, 1))
        _, ys = jax.lax.scan(step, h0, xs)
        y = jnp.swapaxes(ys, 0, 1)
        y_apply_D = y + x * W_D
        y_skip = y_apply_D * _silu(skip)
        return resid + y_skip @ W_out

    def _L0_ffn_ref(hidden_states, router_weight, router_bias, expert_bias):
        import jax, jax.numpy as jnp
        import numpy as np
        TOP_K = 8
        B, S, H = hidden_states.shape
        flat = hidden_states.reshape(B * S, H)
        logits = jnp.einsum('th,eh->te', flat, router_weight) + router_bias
        scores = jax.nn.softmax(logits, axis=-1)
        topk_w, topk_idx = jax.lax.top_k(scores, TOP_K)
        gathered_bias = expert_bias[topk_idx]
        out = flat * jnp.sum(topk_w, axis=-1, keepdims=True) + jnp.einsum('tk,tkh->th', topk_w, gathered_bias)
        return out.reshape(B, S, H)
    x = L0_attn_resid
    x = x + _layernorm(_L0_attn_ref(_layernorm(x, axis=-1), L0_attn_norm_w, L0_attn_W_skip, L0_attn_W_in, L0_attn_conv_w, L0_attn_conv_b, L0_attn_W_delta_1, L0_attn_W_delta_2, L0_attn_b_delta_2, L0_attn_W_B, L0_attn_W_C, L0_attn_A_log, L0_attn_W_D, L0_attn_W_out), axis=-1)
    x = x + _layernorm(_L0_ffn_ref(_layernorm(x, axis=-1), L0_ffn_router_weight, L0_ffn_router_bias, L0_ffn_expert_bias), axis=-1)
    return x

_drawn_inputs = setup_inputs


def setup_inputs(seed=0):
    import zlib

    import numpy as np

    out = dict(_drawn_inputs(seed))
    spreads = {'L0_attn_norm_w': (1.0, 0.2), 'L0_attn_W_D': (1.0, 0.2), 'L0_ffn_router_bias': (0.0, 2.0)}
    factors = {'L0_attn_conv_b': 5.701, 'L0_attn_b_delta_2': 22.238}
    for name, (base, spread) in spreads.items():
        noise = np.random.default_rng([zlib.crc32(name.encode()), seed]).standard_normal(out[name].shape)
        drawn = base * np.exp(spread * noise) if base else spread * noise
        out[name] = jnp.asarray(drawn.astype(out[name].dtype))
    for name, factor in factors.items():
        out[name] = (out[name] * factor).astype(out[name].dtype)
    return out
```

```python
import concourse.bass as bass
from concourse import mybir
from contextlib import ExitStack

P = 128
D = 512
E = 1024
N = 16
DELTA = 128
TAPS = 4
EXPERTS = 64
TOP = 8
BATCH, LEN = 2, 2048
EPS = 1e-5
T = 256
CHUNKS = BATCH * LEN // T
PER_BATCH = LEN // T
TB = T // P
KD = D // P
ET = E // P
HALF = ET // 2
PAIRS = ET // 2
SLOTS = 2 * N
GROUP = 4


class Signal:

    def __init__(self, nc, stack, name, job, per, unit=1):
        self.sem = stack.enter_context(nc.semaphore(name))
        self.job, self.per, self.unit = job, per, unit


class Section:

    def __init__(self, first, jobs):
        self.first, self.jobs, self.seen = first, jobs, {}

    def value(self, signal, step, event):
        while event <= 0:
            step, event = step - 1, event + signal.per
        if step < 0 or signal.job not in self.jobs[step]:
            return 0
        before = sum(signal.job in jobs for jobs in self.jobs[:step])
        return (before * signal.per + event) * signal.unit

    def due(self, engine, signal, step, event):
        value = self.value(signal, step, event)
        key = id(engine), signal.sem.num
        if value <= self.seen.get(key, 0):
            return 0
        self.seen[key] = value
        return value


class Chain:

    def __init__(self, nc, stack, name):
        self.sem, self.count = stack.enter_context(nc.semaphore(name)), 0

    def link(self, engine, instruction):
        self.count += 1
        instruction.then_inc(self.sem, 1)
        engine.wait_ge(self.sem, self.count)


def build(nc, resid, norm_w, w_skip, w_in, conv_w, conv_b, w_delta_1, w_delta_2, b_delta_2, w_b, w_c, a_log,
          w_d, w_out, router_w, router_b, expert_b, out):
    F32 = mybir.dt.float32
    ALU, ACT, AX = mybir.AluOpType, mybir.ActivationFunctionType, mybir.AxisListType
    x_rows = resid.rearrange("b l d -> (b l) d")
    out_rows = out.rearrange("b l d -> (b l) d")
    b_rows = nc.dram_tensor("b_rows", [2, N, T], F32).ap()

    with ExitStack() as stack:
        def sb(name, *shape):
            return stack.enter_context(nc.sbuf_tensor(name, list(shape), F32))

        win, wskip = sb("win", P, KD, E), sb("wskip", P, KD, E)
        wout = sb("wout", P, ET, D)
        wd1, wd2 = sb("wd1", P, ET, DELTA), sb("wd2", P, E)
        wb, wc = sb("wb", P, ET, N), sb("wc", P, ET, N)
        wrouter, ebias = sb("wrouter", P, KD, EXPERTS), sb("ebias", EXPERTS, D)
        neg_a = sb("neg_a", P, ET, N)
        taps, cbias = sb("taps", P, ET, TAPS), sb("cbias", P, ET)
        bdelta, dskip, nw = sb("bdelta", P, ET), sb("dskip", P, ET), sb("nw", P, KD)
        rbias, ones = sb("rbias", 1, EXPERTS), sb("ones", 1, P)
        ident, mhalf = sb("ident", P, P), sb("mhalf", P, TB)
        keep = sb("keep", P, CHUNKS + 2)
        xn = sb("xn", P, TB, D)
        rnt = sb("rnt", P, 2, KD, T)
        xin = sb("xin", P, 2, 2, T + TAPS)
        halo = sb("halo", P, ET, TAPS - 1)
        hv = sb("hv", P, 2, 2, T)
        th = sb("th", P, 2, 2, T)
        x = sb("x", P, ET, T)
        low = sb("low", P, T)
        delta, dx = sb("delta", P, 2, ET, T), sb("dx", P, 2, ET, T)
        b_sb, c_t = sb("b_sb", N, T), sb("c_t", P, 2, TB, N)
        b_all = sb("b_all", P, 2, GROUP, T)
        u, h = sb("u", P, 2, HALF, T), sb("h", P, 2, HALF, T)
        carry = sb("carry", P, N, ET)
        acc = sb("acc", P, 2, TB, E)
        thg, gate = sb("thg", P, 2, 2, T), sb("gate", P, 2, 2, T)
        ys = sb("ys", P, ET, T)
        xp, z = sb("xp", P, TB, D), sb("z", P, TB, D)
        r1k, m1k = sb("r1k", P, 2, TB), sb("m1k", P, 2, TB)
        x1, h2 = sb("x1", P, TB, D), sb("h2", P, TB, D)
        o = gate[:].rearrange("p s e t -> p s (e t)")
        h2t = thg[:].rearrange("p s e (k t) -> p s (e k) t", t=P)
        ex, rem, wt = sb("ex", P, TB, EXPERTS), sb("rem", P, TB, EXPERTS), sb("wt", EXPERTS, TB, P)
        top8 = sb("top8", P, TB, TOP)
        stat6 = sb("stat6", P, TB, 6)
        mvx, mvz, mvh, mvo = (sb(f"mv{n}", P, TB, 2) for n in "xzho")
        small = {n: sb(f"s_{n}", P, TB) for n in
                 ("varx", "r1", "ms", "r2", "s", "ns", "varz", "rz", "nz", "varh", "rh", "nh", "nmx", "se", "rs",
                  "ts", "varo", "ro", "no")}

        da = stack.enter_context(nc.psum_tensor("da", [P, 2, 2, T], F32))
        ht = stack.enter_context(nc.psum_tensor("ht", [P, TB, D], F32))
        work = [stack.enter_context(nc.psum_tensor(f"work{n}", [P, 512], F32)) for n in range(4)]

        signals = []

        def signal(name, job, per, unit=1):
            signals.append(Signal(nc, stack, name, job, per, unit))
            return signals[-1]

        exp_ready = signal("exp_ready", "scan", SLOTS * HALF)
        u_ready = signal("u_ready", "scan", SLOTS)
        scan_done = signal("scan_done", "scan", SLOTS * HALF)
        carry_saved = signal("carry_saved", "scan", SLOTS)
        ht_ready = signal("ht_ready", "scan", SLOTS * TB)
        y_added = signal("y_added", "scan", SLOTS * TB)
        b_loaded = [signal(f"b_loaded{g}", "prep" if g < 2 else "scan", 1, 16) for g in range(N // GROUP)]
        x_loaded = signal("x_loaded", "prep", 1, 16)
        var_x, r1_ready, ms_ready, r2_ready, s_ready = (
            signal(n, "prep", 1) for n in ("var_x", "r1_ready", "ms_ready", "r2_ready", "s_ready"))
        rn_ready = signal("rn_ready", "prep", TB)
        rn_turned, rnt_ready = signal("rn_turned", "prep", 2), signal("rnt_ready", "prep", 2)
        in_done, xin_ready = signal("in_done", "prep", PAIRS), signal("xin_ready", "prep", PAIRS)
        conv_done, halo_saved = signal("conv_done", "prep", PAIRS), signal("halo_saved", "prep", PAIRS)
        th_ready, x_ready = signal("th_ready", "prep", PAIRS), signal("x_ready", "prep", PAIRS)
        norm_kept = signal("norm_kept", "prep", 1)
        low_done, low_ready = signal("low_done", "prep", 1), signal("low_ready", "prep", 1)
        b_ready = signal("b_ready", "prep", 1)
        b_stored = signal("b_stored", "prep", 1, 16)
        c_done, c_ready = signal("c_done", "prep", 1), signal("c_ready", "prep", 1)
        z_done, z_read = signal("zd_done", "prep", PAIRS), signal("zd_read", "prep", PAIRS)
        exp_z, ln_ready = signal("exp_z", "prep", 2), signal("ln_ready", "prep", 2)
        delta_ready, dx_ready = signal("delta_ready", "prep", 2), signal("dx_ready", "prep", 2)
        xd_ready, xd_turned = signal("xd_ready", "prep", PAIRS), signal("xd_turned", "prep", PAIRS)
        acc_init = signal("acc_init", "prep", PAIRS)
        skip_done, thg_ready = signal("skip_done", "mix", PAIRS), signal("thg_ready", "mix", PAIRS)
        gate_ready = signal("gate_ready", "mix", PAIRS)
        y_turned, ys_ready = signal("y_turned", "mix", PAIRS), signal("ys_ready", "mix", PAIRS)
        xp_loaded, z0_ready = signal("xp_loaded", "mix", 1, 16), signal("z0_ready", "mix", TB)
        out_done, z_ready = signal("out_done", "mix", TB), signal("z_ready", "mix", TB)
        var_z, rz_ready, nz_ready, x1_ready = (
            signal(n, "route", 1) for n in ("var_z", "rz_ready", "nz_ready", "x1_ready"))
        var_h, rh_ready, nh_ready = (signal(n, "route", 1) for n in ("var_h", "rh_ready", "nh_ready"))
        zn_ready, h2_ready = signal("zn_ready", "route", TB), signal("h2_ready", "route", TB)
        h2_turned, h2t_ready = signal("h2_turned", "route", TB), signal("h2t_ready", "route", TB)
        logits_done, nmx_ready = signal("logits_done", "route", 1), signal("nmx_ready", "route", 1)
        e_ready, w_ready = signal("e_ready", "route", TB), signal("w_ready", "route", 1)
        w_turned, wt_ready = signal("w_turned", "route", 1), signal("wt_ready", "route", 1)
        eb_done, o_ready = signal("eb_done", "route", TB), signal("o_ready", "route", TB)
        var_o, ro_ready, no_ready = (signal(n, "route", 1) for n in ("var_o", "ro_ready", "no_ready"))
        on_ready, out_ready = signal("on_ready", "route", TB), signal("out_ready", "route", 1)
        out_stored = signal("out_stored", "route", 1, 16)
        dve_chain, act_chain = Chain(nc, stack, "dve_chain"), Chain(nc, stack, "act_chain")
        loads = stack.enter_context(nc.semaphore("loads"))
        a_ready, ident_made = stack.enter_context(nc.semaphore("a_ready")), stack.enter_context(nc.semaphore("ident_made"))
        router_in, router_turned, vectors_ready = (
            stack.enter_context(nc.semaphore(n)) for n in ("router_in", "router_turned", "vectors_ready"))
        numbers = [s.sem.num for s in signals] + [s.num for s in
                   (dve_chain.sem, act_chain.sem, loads, a_ready, ident_made, router_in, router_turned, vectors_ready)]

        def clear_semaphores():
            nc.sync.sem_clear(range(min(numbers), max(numbers) + 1))
            nc.all_engine_barrier(sem_only=True)

        with nc.Block() as block:
            tiles = lambda w: w.rearrange("(k p) n -> p k n", p=P)
            router_rows = x1[0:EXPERTS, 0, :]
            vector_rows = h2[0:KD + (TAPS + 3) * ET, 0, 0:P]
            vectors = [norm_w, conv_b, b_delta_2, w_d] + [conv_w[k, 0] for k in range(TAPS)]
            small_loads, row = [(router_rows, router_w)], 0
            for v in vectors:
                rows_of_v = v.rearrange("(k p) -> k p", p=P)
                small_loads.append((vector_rows[row:row + rows_of_v.shape[0], :], rows_of_v))
                row += rows_of_v.shape[0]
            small_loads += [(neg_a[:], tiles(a_log)), (rbias[:], router_b.unsqueeze(0)), (ebias[:], expert_b),
                            (wb[:], tiles(w_b)), (wc[:], tiles(w_c))]
            large_loads = [(win[:], tiles(w_in)), (wskip[:], tiles(w_skip)), (wout[:], tiles(w_out)),
                           (wd1[:], tiles(w_delta_1)), (wd2[:], w_delta_2)]

            @block.sync
            def _(sp):
                for to, of in small_loads:
                    sp.dma_start(to, of).then_inc(router_in, 16)
                for to, of in large_loads:
                    sp.dma_start(to, of).then_inc(loads, 16)
                sp.wait_ge(router_in, 16 * len(small_loads))
                sp.wait_ge(loads, 16 * len(large_loads))

            @block.gpsimd
            def _(pool):
                nc.gpsimd.memset(ident[:], 0.0).then_inc(ident_made, 1)
                pool.wait_ge(ident_made, 1)
                nc.gpsimd.affine_select(out=ident[:], in_=ident[:], compare_op=ALU.not_equal, fill=1.0, base=0,
                                        pattern=[[-1, P]], channel_multiplier=1).then_inc(ident_made, 1)
                nc.gpsimd.memset(mhalf[:], -0.5)
                nc.gpsimd.memset(ones[:], 1.0)
                nc.gpsimd.memset(carry[:], 0.0)
                nc.gpsimd.memset(halo[:], 0.0)

            @block.scalar
            def _(act):
                act.wait_ge(router_in, 16 * len(small_loads))
                nc.scalar.activation(neg_a[:], neg_a[:], ACT.Exp).then_inc(a_ready, 1)
                act.wait_ge(router_turned, 1)
                nc.scalar.activation(wrouter[:].rearrange("p k e -> p (k e)"), work[0][:, 0:KD * EXPERTS], ACT.Copy)
                turned, at = work[1], 0
                for to, scale in ((nw[:], 1.0), (cbias[:], 0.5), (bdelta[:], 1.0), (dskip[:], 1.0)):
                    nc.scalar.activation(to, turned[:, at:at + to.shape[1]], ACT.Copy,
                                         scale=scale).then_inc(vectors_ready, 1)
                    at += to.shape[1]
                nc.scalar.activation(taps[:], turned[:, at:at + TAPS * ET].rearrange("p (k e) -> p e k", k=TAPS),
                                     ACT.Copy, scale=0.5)
                act.wait_ge(vectors_ready, 1)
                act.wait_ge(loads, 16 * len(large_loads))
                for k in range(KD):
                    nc.scalar.activation(wskip[:, k, :], wskip[:, k, :], ACT.Copy, scale=nw[:, k:k + 1])

            @block.vector
            def _(dve):
                dve_chain.link(dve, nc.vector.memset(keep[:], 1.0))
                dve.wait_ge(router_in, 16 * len(small_loads))
                for j in range(0, CHUNKS + 2, PER_BATCH):
                    dve_chain.link(dve, nc.vector.memset(keep[:, j:j + 1], 0.0))
                dve.wait_ge(a_ready, 1)
                nc.vector.tensor_scalar(neg_a[:], neg_a[:], -1.0, None, ALU.mult)
                dve.wait_ge(loads, 16 * len(large_loads))
                dve.wait_ge(vectors_ready, 1)
                nc.vector.tensor_scalar(wout[:], wout[:], 0.5, None, ALU.mult)
                for k in range(KD):
                    nc.vector.tensor_scalar(win[:, k, :], win[:, k, :], nw[:, k:k + 1], None, ALU.mult)

            @block.tensor
            def _(pe):
                pe.wait_ge(router_in, 16 * len(small_loads))
                pe.wait_ge(ident_made, 2)
                for k in range(KD):
                    nc.tensor.transpose(work[0][:, k * EXPERTS:(k + 1) * EXPERTS],
                                               router_rows[:, k * P:(k + 1) * P], ident[0:EXPERTS, 0:EXPERTS])
                nc.tensor.transpose(work[1][:, 0:vector_rows.shape[0]], vector_rows,
                                    ident[0:vector_rows.shape[0], 0:vector_rows.shape[0]]).then_inc(router_turned, 1)
        clear_semaphores()

        def pair_bank(p):
            return work[1 + p % 2]

        def section(first, jobs, parity):
            sec = Section(first, jobs)
            dve_chain.count = act_chain.count = 0
            due = sec.due

            def rows(chunk):
                return bass.ds(chunk * T, T)

            def per_block(ap):
                return ap.rearrange("(b p) d -> p b d", p=P)

            with nc.Block() as block:
                @block.sync
                def _(sp):
                    def load_b(side, group):
                        src = b_rows[side, group * GROUP:(group + 1) * GROUP].unsqueeze(0)
                        sp.dma_start(b_all[:, group % 2], src.to_broadcast([P, GROUP, T])).then_inc(
                            b_loaded[group].sem, 16)

                    for t, jobs_now in enumerate(jobs):
                        i, now = first + t, (parity + t) % 2
                        for s in range(SLOTS):
                            if "prep" in jobs_now and s == 0:
                                if v := due(sp, rn_turned, t - 1, 2):
                                    sp.wait_ge(rn_turned.sem, v)
                                sp.dma_start(xn[:], per_block(x_rows[rows(i + 1), :])).then_inc(x_loaded.sem, 16)
                            if "mix" in jobs_now and s == 8:
                                if v := due(sp, x1_ready, t, 1):
                                    sp.wait_ge(x1_ready.sem, v)
                                sp.dma_start(xp[:], per_block(x_rows[rows(i - 1), :])).then_inc(xp_loaded.sem, 16)
                            if "scan" in jobs_now and s in (8, 16):
                                group = 1 + s // 8
                                if v := due(sp, u_ready, t, (group - 1) * 2 * GROUP):
                                    sp.wait_ge(u_ready.sem, v)
                                load_b(now, group)
                            if "prep" in jobs_now and s == 27:
                                if v := due(sp, b_ready, t, 1):
                                    sp.wait_ge(b_ready.sem, v)
                                for done in b_loaded:
                                    if v := due(sp, done, t - 1 if done.job == "scan" else t - 2, 1):
                                        sp.wait_ge(done.sem, v)
                                sp.dma_start(b_rows[1 - now], b_sb[:]).then_inc(b_stored.sem, 16)
                            if "prep" in jobs_now and s == 28:
                                if v := due(sp, b_stored, t, 1):
                                    sp.wait_ge(b_stored.sem, v)
                                if v := due(sp, u_ready, t, 3 * 2 * GROUP):
                                    sp.wait_ge(u_ready.sem, v)
                                load_b(1 - now, 0)
                            if "route" in jobs_now and s == 30:
                                if v := due(sp, out_ready, t, 1):
                                    sp.wait_ge(out_ready.sem, v)
                                sp.dma_start(per_block(out_rows[rows(i - 2), :]), o).then_inc(out_stored.sem, 16)
                        if "prep" in jobs_now:
                            if v := due(sp, u_ready, t, SLOTS):
                                sp.wait_ge(u_ready.sem, v)
                            load_b(1 - now, 1)
                    for done in (x_loaded, xp_loaded, *b_loaded, b_stored, out_stored):
                        for t in range(len(jobs)):
                            if v := due(sp, done, t, done.per):
                                sp.wait_ge(done.sem, v)

                @block.gpsimd
                def _(pool):
                    def rstd(to, var):
                        return nc.gpsimd.tensor_tensor(small[to][:], small[var][:], mhalf[:], ALU.pow)

                    for t, jobs_now in enumerate(jobs):
                        now, other = (parity + t) % 2, (parity + t + 1) % 2
                        for s in range(SLOTS):
                            if "scan" in jobs_now:
                                n, eh = s // 2, s % 2
                                group = n // GROUP
                                if v := due(pool, scan_done, t, HALF * (s - 1)):
                                    pool.wait_ge(scan_done.sem, v)
                                if v := due(pool, b_loaded[group], t - 1 if group < 2 else t, 1):
                                    pool.wait_ge(b_loaded[group].sem, v)
                                if v := due(pool, dx_ready, t - 1, eh + 1):
                                    pool.wait_ge(dx_ready.sem, v)
                                b_row = b_all[:, group % 2, n % GROUP:n % GROUP + 1, :]
                                nc.gpsimd.tensor_tensor(u[:, s % 2], dx[:, now, eh * HALF:(eh + 1) * HALF, :],
                                                        b_row.to_broadcast([P, HALF, T]),
                                                        ALU.mult).then_inc(u_ready.sem, 1)
                            if "prep" in jobs_now:
                                if s == 2:
                                    if v := due(pool, var_x, t, 1):
                                        pool.wait_ge(var_x.sem, v)
                                    rstd("r1", "varx").then_inc(r1_ready.sem, 1)
                                if s == 4:
                                    if v := due(pool, ms_ready, t, 1):
                                        pool.wait_ge(ms_ready.sem, v)
                                    rstd("r2", "ms").then_inc(r2_ready.sem, 1)
                                if s == 31:
                                    for eh in range(2):
                                        part = slice(eh * HALF, (eh + 1) * HALF)
                                        if v := due(pool, delta_ready, t, eh + 1):
                                            pool.wait_ge(delta_ready.sem, v)
                                        nc.gpsimd.tensor_tensor(dx[:, other, part], delta[:, other, part], x[:, part],
                                                                ALU.mult).then_inc(dx_ready.sem, 1)
                            if "route" in jobs_now:
                                if s == 1:
                                    if v := due(pool, var_z, t, 1):
                                        pool.wait_ge(var_z.sem, v)
                                    rstd("rz", "varz").then_inc(rz_ready.sem, 1)
                                if s == 4:
                                    if v := due(pool, zn_ready, t, TB):
                                        pool.wait_ge(zn_ready.sem, v)
                                    if v := due(pool, xp_loaded, t - 1, 1):
                                        pool.wait_ge(xp_loaded.sem, v)
                                    if v := due(pool, out_ready, t - 1, 1):
                                        pool.wait_ge(out_ready.sem, v)
                                    nc.gpsimd.tensor_tensor(x1[:], xp[:], z[:], ALU.add).then_inc(x1_ready.sem, 1)
                                if s == 7:
                                    if v := due(pool, var_h, t, 1):
                                        pool.wait_ge(var_h.sem, v)
                                    rstd("rh", "varh").then_inc(rh_ready.sem, 1)
                                if s == 26:
                                    if v := due(pool, var_o, t, 1):
                                        pool.wait_ge(var_o.sem, v)
                                    rstd("ro", "varo").then_inc(ro_ready.sem, 1)
                                if s == 29:
                                    if v := due(pool, on_ready, t, TB):
                                        pool.wait_ge(on_ready.sem, v)
                                    if v := due(pool, x1_ready, t, 1):
                                        pool.wait_ge(x1_ready.sem, v)
                                    nc.gpsimd.tensor_tensor(o, x1[:], o, ALU.add).then_inc(out_ready.sem, 1)

                @block.scalar
                def _(act):
                    def scaled(to, of, scale, bias):
                        return nc.scalar.activation(to, of, ACT.Identity, bias=bias, scale=scale)

                    for t, jobs_now in enumerate(jobs):
                        now, other = (parity + t) % 2, (parity + t + 1) % 2
                        for s in range(SLOTS):
                            if "scan" in jobs_now:
                                n, eh = s // 2, s % 2
                                if v := due(act, delta_ready, t - 1, eh + 1):
                                    act.wait_ge(delta_ready.sem, v)
                                for q in range(HALF):
                                    et = eh * HALF + q
                                    if v := due(act, scan_done, t, HALF * (s - 1) + q // 2 * 2 + 2):
                                        act.wait_ge(scan_done.sem, v)
                                    nc.scalar.activation(da[:, q // 2, q % 2, :], delta[:, now, et, :], ACT.Exp,
                                                         scale=neg_a[:, et, n:n + 1]).then_inc(exp_ready.sem, 1)
                            if "prep" in jobs_now:
                                if s == 6:
                                    if v := due(act, s_ready, t, 1):
                                        act.wait_ge(s_ready.sem, v)
                                    for b in range(TB):
                                        scaled(xn[:, b], xn[:, b], small["s"][:, b:b + 1],
                                               small["ns"][:, b:b + 1]).then_inc(rn_ready.sem, 1)
                                if s in (9, 11):
                                    k = s - 9
                                    if v := due(act, rn_turned, t, k // 2 + 1):
                                        act.wait_ge(rn_turned.sem, v)
                                    if v := due(act, skip_done, t, PAIRS):
                                        act.wait_ge(skip_done.sem, v)
                                    if v := due(act, in_done, t - 2, PAIRS):
                                        act.wait_ge(in_done.sem, v)
                                    nc.scalar.activation(rnt[:, other, k:k + 2, :].rearrange("p k t -> p (k t)"),
                                                         pair_bank(k // 2)[:], ACT.Copy).then_inc(rnt_ready.sem, 1)
                                for p in range(PAIRS):
                                    if s == 14 + 2 * p:
                                        if v := due(act, in_done, t, p + 1):
                                            act.wait_ge(in_done.sem, v)
                                        if v := due(act, halo_saved, t, p - 1):
                                            act.wait_ge(halo_saved.sem, v)
                                        if v := due(act, x_ready, t, p - 1):
                                            act.wait_ge(x_ready.sem, v)
                                        if v := due(act, xd_turned, t - 1, PAIRS):
                                            act.wait_ge(xd_turned.sem, v)
                                        bank = pair_bank(p)[:].rearrange("p (e t) -> p e t", e=2)
                                        nc.scalar.activation(xin[:, p % 2, :, TAPS - 1:TAPS - 1 + T], bank, ACT.Copy)
                                        for e in range(2):
                                            et = 2 * p + e
                                            last = scaled(hv[:, p % 2, e, :], bank[:, e, :],
                                                          taps[:, et, TAPS - 1:TAPS], cbias[:, et:et + 1])
                                        last.then_inc(xin_ready.sem, 1)
                                    if s == 16 + 2 * p:
                                        if v := due(act, conv_done, t, p + 1):
                                            act.wait_ge(conv_done.sem, v)
                                        if v := due(act, x_ready, t, p - 1):
                                            act.wait_ge(x_ready.sem, v)
                                        nc.scalar.activation(th[:, p % 2], hv[:, p % 2],
                                                             ACT.Tanh).then_inc(th_ready.sem, 1)
                                    if s == (24, 25, 27, 29)[p]:
                                        if v := due(act, x_ready, t, PAIRS):
                                            act.wait_ge(x_ready.sem, v)
                                        if v := due(act, xd_turned, t, p - 1):
                                            act.wait_ge(xd_turned.sem, v)
                                        for e in range(2):
                                            et = 2 * p + e
                                            last = nc.scalar.activation(hv[:, p % 2, e, :], x[:, et, :], ACT.Copy,
                                                                        scale=dskip[:, et:et + 1])
                                        last.then_inc(xd_ready.sem, 1)
                                    if s == (26, 28, 31, 31)[p]:
                                        if v := due(act, xd_turned, t, p + 1):
                                            act.wait_ge(xd_turned.sem, v)
                                        if v := due(act, y_turned, t, PAIRS):
                                            act.wait_ge(y_turned.sem, v)
                                        bank = work[(3, 3, 0, 3)[p]][:].rearrange("p (b e) -> p b e", b=TB)
                                        nc.scalar.activation(acc[:, other, :, 2 * p * P:2 * (p + 1) * P], bank,
                                                             ACT.Copy).then_inc(acc_init.sem, 1)
                                    if s == 27 + p:
                                        if v := due(act, z_done, t, p + 1):
                                            act.wait_ge(z_done.sem, v)
                                        if v := due(act, exp_ready, t - 1, SLOTS * HALF):
                                            act.wait_ge(exp_ready.sem, v)
                                        if v := due(act, u_ready, t - 1, SLOTS):
                                            act.wait_ge(u_ready.sem, v)
                                        for e in range(2):
                                            et = 2 * p + e
                                            v = pair_bank(p)[:, e * T:(e + 1) * T]
                                            nc.scalar.activation(delta[:, other, et, :], v, ACT.Relu,
                                                                 bias=bdelta[:, et:et + 1])
                                            last = nc.scalar.activation(dx[:, other, et, :], v, ACT.Abs,
                                                                        bias=bdelta[:, et:et + 1])
                                        last.then_inc(z_read.sem, 1)
                                if s == 25:
                                    if v := due(act, low_done, t, 1):
                                        act.wait_ge(low_done.sem, v)
                                    if v := due(act, z_done, t - 1, PAIRS):
                                        act.wait_ge(z_done.sem, v)
                                    nc.scalar.activation(low[:], work[1][:, 0:T], ACT.Copy).then_inc(low_ready.sem, 1)
                                if s == 26:
                                    if v := due(act, c_done, t, 1):
                                        act.wait_ge(c_done.sem, v)
                                    if v := due(act, b_stored, t - 1, 1):
                                        act.wait_ge(b_stored.sem, v)
                                    nc.scalar.activation(b_sb[:], work[2][0:N, 0:T], ACT.Copy).then_inc(b_ready.sem, 1)
                                    if v := due(act, y_added, t - 1, SLOTS * TB):
                                        act.wait_ge(y_added.sem, v)
                                    nc.scalar.activation(c_t[:, other].rearrange("p b n -> p (b n)"),
                                                         work[2][:, T:T + TB * N], ACT.Copy).then_inc(c_ready.sem, 1)
                                if s == 31:
                                    if v := due(act, z_read, t, PAIRS):
                                        act.wait_ge(z_read.sem, v)
                                    for eh in range(2):
                                        part = dx[:, other, eh * HALF:(eh + 1) * HALF]
                                        nc.scalar.activation(part, part, ACT.Exp, scale=-1.0).then_inc(exp_z.sem, 1)
                                    for eh in range(2):
                                        part = dx[:, other, eh * HALF:(eh + 1) * HALF]
                                        if v := due(act, exp_z, t, eh + 1):
                                            act.wait_ge(exp_z.sem, v)
                                        nc.scalar.activation(part, part, ACT.Ln, bias=1.0).then_inc(ln_ready.sem, 1)
                            if "mix" in jobs_now:
                                for p in range(PAIRS):
                                    if s == 2 * p + 2:
                                        if v := due(act, skip_done, t, p + 1):
                                            act.wait_ge(skip_done.sem, v)
                                        if v := due(act, gate_ready, t, p - 1):
                                            act.wait_ge(gate_ready.sem, v)
                                        if v := due(act, logits_done, t - 1, 1):
                                            act.wait_ge(logits_done.sem, v)
                                        nc.scalar.activation(thg[:, p % 2].rearrange("p e t -> p (e t)"),
                                                             pair_bank(p)[:], ACT.Tanh,
                                                             scale=0.5).then_inc(thg_ready.sem, 1)
                                if s == 12:
                                    if v := due(act, xp_loaded, t, 1):
                                        act.wait_ge(xp_loaded.sem, v)
                                    if v := due(act, norm_kept, t - 2, 1):
                                        act.wait_ge(norm_kept.sem, v)
                                    if v := due(act, x1_ready, t, 1):
                                        act.wait_ge(x1_ready.sem, v)
                                    for b in range(TB):
                                        scaled(z[:, b], xp[:, b], r1k[:, other, b:b + 1],
                                               m1k[:, other, b:b + 1]).then_inc(z0_ready.sem, 1)
                            if "route" in jobs_now:
                                if s == 3:
                                    if v := due(act, nz_ready, t, 1):
                                        act.wait_ge(nz_ready.sem, v)
                                    for b in range(TB):
                                        scaled(z[:, b], z[:, b], small["rz"][:, b:b + 1],
                                               small["nz"][:, b:b + 1]).then_inc(zn_ready.sem, 1)
                                if s == 9:
                                    if v := due(act, nh_ready, t, 1):
                                        act.wait_ge(nh_ready.sem, v)
                                    if v := due(act, o_ready, t - 1, TB):
                                        act.wait_ge(o_ready.sem, v)
                                    for b in range(TB):
                                        scaled(h2[:, b], x1[:, b], small["rh"][:, b:b + 1],
                                               small["nh"][:, b:b + 1]).then_inc(h2_ready.sem, 1)
                                if s in (11, 13):
                                    b = (s - 11) // 2
                                    if v := due(act, h2_turned, t, b + 1):
                                        act.wait_ge(h2_turned.sem, v)
                                    if v := due(act, logits_done, t - 1, 1):
                                        act.wait_ge(logits_done.sem, v)
                                    if v := due(act, gate_ready, t, PAIRS):
                                        act.wait_ge(gate_ready.sem, v)
                                    nc.scalar.activation(h2t[:, b].rearrange("p k t -> p (k t)"), work[3][:],
                                                         ACT.Copy).then_inc(h2t_ready.sem, 1)
                                if s == 16:
                                    if v := due(act, nmx_ready, t, 1):
                                        act.wait_ge(nmx_ready.sem, v)
                                    if v := due(act, w_turned, t - 1, 1):
                                        act.wait_ge(w_turned.sem, v)
                                    for b in range(TB):
                                        nc.scalar.activation(ex[:, b], work[3][:, b * EXPERTS:(b + 1) * EXPERTS],
                                                             ACT.Exp, bias=small["nmx"][:, b:b + 1],
                                                             accum_out=small["se"][:, b:b + 1]).then_inc(e_ready.sem, 1)
                                if s == 20:
                                    if v := due(act, w_turned, t, 1):
                                        act.wait_ge(w_turned.sem, v)
                                    if v := due(act, eb_done, t - 1, TB):
                                        act.wait_ge(eb_done.sem, v)
                                    nc.scalar.activation(wt[:].rearrange("e b t -> e (b t)"),
                                                         work[3][0:EXPERTS, 0:TB * P],
                                                         ACT.Copy).then_inc(wt_ready.sem, 1)
                                if s == 28:
                                    if v := due(act, no_ready, t, 1):
                                        act.wait_ge(no_ready.sem, v)
                                    for b in range(TB):
                                        scaled(o[:, b], o[:, b], small["ro"][:, b:b + 1],
                                               small["no"][:, b:b + 1]).then_inc(on_ready.sem, 1)

                @block.vector
                def _(dve):
                    def link(instruction):
                        dve_chain.link(dve, instruction)

                    def moments(of, mv, var, ready):
                        for b in range(TB):
                            last = nc.vector.bn_stats(stat6[:, b], of[:, b])
                        link(last)
                        for b in range(TB):
                            last = nc.vector.bn_aggr(mv[:, b], stat6[:, b])
                        link(last)
                        nc.vector.tensor_scalar(small[var][:], mv[:, :, 1], EPS, None, ALU.add).then_inc(ready.sem, 1)

                    def minus_mean_times(to, mv, r):
                        return nc.vector.scalar_tensor_tensor(out=to, in0=mv[:, :, 0], scalar=-1.0, in1=r,
                                                              op0=ALU.mult, op1=ALU.mult)

                    def finish(t, s):
                        now, n, eh = (parity + t) % 2, s // 2, s % 2
                        if v := due(dve, scan_done, t, HALF * (s + 1)):
                            dve.wait_ge(scan_done.sem, v)
                        nc.vector.tensor_tensor(carry[:, n, eh * HALF:(eh + 1) * HALF], h[:, s % 2, :, T - 1],
                                                keep[:, bass.ds(first + t + 1, 1)].to_broadcast([P, HALF]),
                                                ALU.mult).then_inc(carry_saved.sem, 1)
                        if v := due(dve, c_ready, t - 1, 1):
                            dve.wait_ge(c_ready.sem, v)
                        if v := due(dve, acc_init, t - 1, PAIRS):
                            dve.wait_ge(acc_init.sem, v)
                        for b in range(TB):
                            y = acc[:, now, b, eh * D:(eh + 1) * D]
                            if v := due(dve, ht_ready, t, TB * s + b + 1):
                                dve.wait_ge(ht_ready.sem, v)
                            if v := due(dve, y_added, t, TB * (s - 2) + b + 1):
                                dve.wait_ge(y_added.sem, v)
                            nc.vector.scalar_tensor_tensor(out=y, in0=ht[:, b], scalar=c_t[:, now, b, n:n + 1], in1=y,
                                                           op0=ALU.mult, op1=ALU.add).then_inc(y_added.sem, 1)

                    unfinished = None
                    for t, jobs_now in enumerate(jobs):
                        now, other = (parity + t) % 2, (parity + t + 1) % 2
                        for s in range(SLOTS):
                            if "scan" in jobs_now:
                                n, eh = s // 2, s % 2
                                if v := due(dve, u_ready, t, s + 1):
                                    dve.wait_ge(u_ready.sem, v)
                                if v := due(dve, ht_ready, t, TB * (s - 1)):
                                    dve.wait_ge(ht_ready.sem, v)
                                if v := due(dve, carry_saved, t, s - 1):
                                    dve.wait_ge(carry_saved.sem, v)
                                for q in range(HALF):
                                    et = eh * HALF + q
                                    if v := due(dve, exp_ready, t, HALF * s + q // 2 * 2 + 2):
                                        dve.wait_ge(exp_ready.sem, v)
                                    nc.vector.tensor_tensor_scan(h[:, s % 2, q, :], da[:, q // 2, q % 2, :],
                                                                 u[:, s % 2, q, :], carry[:, n, et:et + 1],
                                                                 ALU.mult, ALU.add).then_inc(scan_done.sem, 1)
                                if unfinished:
                                    finish(*unfinished)
                                unfinished = t, s
                            elif unfinished:
                                finish(*unfinished)
                                unfinished = None
                            if "prep" in jobs_now:
                                if s == 1:
                                    if v := due(dve, x_loaded, t, 1):
                                        dve.wait_ge(x_loaded.sem, v)
                                    moments(xn, mvx, "varx", var_x)
                                if s == 3:
                                    if v := due(dve, r1_ready, t, 1):
                                        dve.wait_ge(r1_ready.sem, v)
                                    link(nc.vector.tensor_tensor(small["ms"][:], small["r1"][:], small["r1"][:],
                                                                 ALU.mult))
                                    link(nc.vector.tensor_tensor(small["ms"][:], small["ms"][:], mvx[:, :, 1],
                                                                 ALU.mult))
                                    nc.vector.tensor_scalar(small["ms"][:], small["ms"][:], EPS, None,
                                                            ALU.add).then_inc(ms_ready.sem, 1)
                                if s == 5:
                                    if v := due(dve, r2_ready, t, 1):
                                        dve.wait_ge(r2_ready.sem, v)
                                    link(nc.vector.tensor_tensor(small["s"][:], small["r1"][:], small["r2"][:],
                                                                 ALU.mult))
                                    minus_mean_times(small["ns"][:], mvx, small["s"][:]).then_inc(s_ready.sem, 1)
                                if s == 14:
                                    if v := due(dve, z0_ready, t, TB):
                                        dve.wait_ge(z0_ready.sem, v)
                                    nc.vector.tensor_copy(r1k[:, other], small["r1"][:])
                                    minus_mean_times(m1k[:, other], mvx, small["r1"][:]).then_inc(norm_kept.sem, 1)
                                for p in range(PAIRS):
                                    if s == 15 + 2 * p:
                                        xi = xin[:, p % 2]
                                        if v := due(dve, xin_ready, t, p + 1):
                                            dve.wait_ge(xin_ready.sem, v)
                                        if v := due(dve, halo_saved, t - 1, p + 1):
                                            dve.wait_ge(halo_saved.sem, v)
                                        link(nc.vector.tensor_copy(xi[:, :, 0:TAPS - 1], halo[:, 2 * p:2 * p + 2, :]))
                                        for k in range(TAPS - 1):
                                            for e in range(2):
                                                v = hv[:, p % 2, e, :]
                                                last = nc.vector.scalar_tensor_tensor(
                                                    out=v, in0=xi[:, e, k:k + T], scalar=taps[:, 2 * p + e, k:k + 1],
                                                    in1=v, op0=ALU.mult, op1=ALU.add)
                                            if k < TAPS - 2:
                                                link(last)
                                        last.then_inc(conv_done.sem, 1)
                                        nc.vector.tensor_tensor(
                                            halo[:, 2 * p:2 * p + 2, :], xi[:, :, T:T + TAPS - 1],
                                            keep[:, bass.ds(first + t + 2, 1)].unsqueeze(1)
                                            .to_broadcast([P, 2, TAPS - 1]), ALU.mult).then_inc(halo_saved.sem, 1)
                                    if s == 17 + 2 * p:
                                        if v := due(dve, th_ready, t, p + 1):
                                            dve.wait_ge(th_ready.sem, v)
                                        if v := due(dve, dx_ready, t - 1, 2):
                                            dve.wait_ge(dx_ready.sem, v)
                                        if v := due(dve, c_done, t - 1, 1):
                                            dve.wait_ge(c_done.sem, v)
                                        if v := due(dve, xd_ready, t - 1, PAIRS):
                                            dve.wait_ge(xd_ready.sem, v)
                                        nc.vector.scalar_tensor_tensor(
                                            out=x[:, 2 * p:2 * p + 2, :], in0=th[:, p % 2], scalar=1.0,
                                            in1=hv[:, p % 2], op0=ALU.add, op1=ALU.mult).then_inc(x_ready.sem, 1)
                                if s == 31:
                                    for eh in range(2):
                                        part = slice(eh * HALF, (eh + 1) * HALF)
                                        if v := due(dve, ln_ready, t, eh + 1):
                                            dve.wait_ge(ln_ready.sem, v)
                                        nc.vector.tensor_tensor(delta[:, other, part], delta[:, other, part],
                                                                dx[:, other, part],
                                                                ALU.add).then_inc(delta_ready.sem, 1)
                            if "mix" in jobs_now:
                                for p in range(PAIRS):
                                    if s == 2 * p + 3:
                                        if v := due(dve, thg_ready, t, p + 1):
                                            dve.wait_ge(thg_ready.sem, v)
                                        if v := due(dve, ys_ready, t, p - 1):
                                            dve.wait_ge(ys_ready.sem, v)
                                        if v := due(dve, out_stored, t - 1, 1):
                                            dve.wait_ge(out_stored.sem, v)
                                        nc.vector.scalar_tensor_tensor(
                                            out=gate[:, p % 2].rearrange("p e t -> p (e t)"),
                                            in0=thg[:, p % 2].rearrange("p e t -> p (e t)"), scalar=1.0,
                                            in1=pair_bank(p)[:], op0=ALU.add,
                                            op1=ALU.mult).then_inc(gate_ready.sem, 1)
                                    if s == 2 * p + 4:
                                        if v := due(dve, y_turned, t, p + 1):
                                            dve.wait_ge(y_turned.sem, v)
                                        if v := due(dve, gate_ready, t, p + 1):
                                            dve.wait_ge(gate_ready.sem, v)
                                        if v := due(dve, out_done, t - 1, TB):
                                            dve.wait_ge(out_done.sem, v)
                                        nc.vector.tensor_tensor(
                                            ys[:, 2 * p:2 * p + 2, :].rearrange("p e t -> p (e t)"), work[0][:],
                                            gate[:, p % 2].rearrange("p e t -> p (e t)"),
                                            ALU.mult).then_inc(ys_ready.sem, 1)
                                if s in (19, 28):
                                    b = (s - 19) // 9
                                    if v := due(dve, out_done, t, b + 1):
                                        dve.wait_ge(out_done.sem, v)
                                    if v := due(dve, z0_ready, t, TB):
                                        dve.wait_ge(z0_ready.sem, v)
                                    nc.vector.tensor_tensor(z[:, b], work[0][:], z[:, b],
                                                            ALU.add).then_inc(z_ready.sem, 1)
                            if "route" in jobs_now:
                                if s == 0:
                                    if v := due(dve, z_ready, t - 1, TB):
                                        dve.wait_ge(z_ready.sem, v)
                                    moments(z, mvz, "varz", var_z)
                                if s == 2:
                                    if v := due(dve, rz_ready, t, 1):
                                        dve.wait_ge(rz_ready.sem, v)
                                    minus_mean_times(small["nz"][:], mvz, small["rz"][:]).then_inc(nz_ready.sem, 1)
                                if s == 6:
                                    if v := due(dve, x1_ready, t, 1):
                                        dve.wait_ge(x1_ready.sem, v)
                                    moments(x1, mvh, "varh", var_h)
                                if s == 8:
                                    if v := due(dve, rh_ready, t, 1):
                                        dve.wait_ge(rh_ready.sem, v)
                                    minus_mean_times(small["nh"][:], mvh, small["rh"][:]).then_inc(nh_ready.sem, 1)
                                if s == 15:
                                    if v := due(dve, logits_done, t, 1):
                                        dve.wait_ge(logits_done.sem, v)
                                    link(nc.vector.tensor_reduce(
                                        small["nmx"][:],
                                        work[3][:, 0:TB * EXPERTS].rearrange("p (b e) -> p b e", b=TB),
                                        axis=AX.X, op=ALU.max))
                                    nc.vector.tensor_scalar(small["nmx"][:], small["nmx"][:], -1.0, None,
                                                            ALU.mult).then_inc(nmx_ready.sem, 1)
                                if s == 17:
                                    if v := due(dve, e_ready, t, TB):
                                        dve.wait_ge(e_ready.sem, v)
                                    for b in range(TB):
                                        last = nc.vector.max(top8[:, b], ex[:, b])
                                    link(last)
                                    for b in range(TB):
                                        nc.vector.match_replace(out=rem[:, b], in_to_replace=top8[:, b],
                                                                in_values=ex[:, b], imm_value=0.0)
                                    nc.vector.tensor_reduce(small["ts"][:], top8[:], axis=AX.X, op=ALU.add)
                                    link(nc.vector.reciprocal(small["rs"][:], small["se"][:]))
                                    nc.vector.tensor_tensor(small["ts"][:], small["ts"][:], small["rs"][:], ALU.mult)
                                    link(nc.vector.tensor_tensor(rem[:], ex[:], rem[:], ALU.subtract))
                                    nc.vector.tensor_tensor(ex[:], rem[:],
                                                            small["rs"][:].unsqueeze(2)
                                                            .to_broadcast([P, TB, EXPERTS]),
                                                            ALU.mult).then_inc(w_ready.sem, 1)
                                if s in (22, 24):
                                    b = (s - 22) // 2
                                    if v := due(dve, eb_done, t, b + 1):
                                        dve.wait_ge(eb_done.sem, v)
                                    if v := due(dve, w_ready, t, 1):
                                        dve.wait_ge(w_ready.sem, v)
                                    if v := due(dve, ys_ready, t, PAIRS):
                                        dve.wait_ge(ys_ready.sem, v)
                                    if v := due(dve, out_stored, t - 1, 1):
                                        dve.wait_ge(out_stored.sem, v)
                                    nc.vector.scalar_tensor_tensor(out=o[:, b], in0=h2[:, b],
                                                                   scalar=small["ts"][:, b:b + 1], in1=work[3][:],
                                                                   op0=ALU.mult,
                                                                   op1=ALU.add).then_inc(o_ready.sem, 1)
                                if s == 25:
                                    if v := due(dve, o_ready, t, TB):
                                        dve.wait_ge(o_ready.sem, v)
                                    moments(o, mvo, "varo", var_o)
                                if s == 27:
                                    if v := due(dve, ro_ready, t, 1):
                                        dve.wait_ge(ro_ready.sem, v)
                                    minus_mean_times(small["no"][:], mvo, small["ro"][:]).then_inc(no_ready.sem, 1)
                    if unfinished:
                        finish(*unfinished)

                @block.tensor
                def _(pe):
                    matmul, transpose = nc.tensor.matmul, nc.tensor.transpose
                    for t, jobs_now in enumerate(jobs):
                        now, other = (parity + t) % 2, (parity + t + 1) % 2
                        for s in range(SLOTS):
                            if "scan" in jobs_now:
                                if v := due(pe, scan_done, t, HALF * (s + 1)):
                                    pe.wait_ge(scan_done.sem, v)
                                for b in range(TB):
                                    if v := due(pe, y_added, t, TB * (s - 1) + b + 1):
                                        pe.wait_ge(y_added.sem, v)
                                    for q in range(HALF):
                                        last = transpose(ht[:, b, q * P:(q + 1) * P],
                                                         h[:, s % 2, q, b * P:(b + 1) * P], ident[:])
                                    last.then_inc(ht_ready.sem, 1)
                            if "prep" in jobs_now:
                                if s in (8, 10):
                                    k0 = s - 8
                                    if v := due(pe, rn_ready, t, TB):
                                        pe.wait_ge(rn_ready.sem, v)
                                    if v := due(pe, gate_ready, t, 3 + k0 // 2):
                                        pe.wait_ge(gate_ready.sem, v)
                                    if v := due(pe, z_read, t - 1, PAIRS):
                                        pe.wait_ge(z_read.sem, v)
                                    for k in range(2):
                                        for b in range(TB):
                                            last = transpose(pair_bank(k0 // 2)[:, k * T + b * P:k * T + (b + 1) * P],
                                                             xn[:, b, (k0 + k) * P:(k0 + k + 1) * P], ident[:])
                                    last.then_inc(rn_turned.sem, 1)
                                for p in range(PAIRS):
                                    if s in (12 + 2 * p, 13 + 2 * p):
                                        e = s % 2
                                        if v := due(pe, rnt_ready, t, 2):
                                            pe.wait_ge(rnt_ready.sem, v)
                                        if v := due(pe, xin_ready, t, p - 1):
                                            pe.wait_ge(xin_ready.sem, v)
                                        for k in range(KD):
                                            last = matmul(pair_bank(p)[:, e * T:(e + 1) * T],
                                                          win[:, k, (2 * p + e) * P:(2 * p + e + 1) * P],
                                                          rnt[:, other, k, :], start=(k == 0), stop=(k == KD - 1))
                                        if e == 1:
                                            last.then_inc(in_done.sem, 1)
                                    if s == (19, 20, 22, 24)[p]:
                                        if v := due(pe, x_ready, t, p + 1):
                                            pe.wait_ge(x_ready.sem, v)
                                        if v := due(pe, xin_ready, t, 3):
                                            pe.wait_ge(xin_ready.sem, v)
                                        for et in (2 * p, 2 * p + 1):
                                            last = matmul(work[1][:, 0:T], wd1[:, et, :], x[:, et, :],
                                                          start=(et == 0), stop=(et == ET - 1))
                                        if p == PAIRS - 1:
                                            last.then_inc(low_done.sem, 1)
                                    if s == 21 + p:
                                        if v := due(pe, x_ready, t, p + 1):
                                            pe.wait_ge(x_ready.sem, v)
                                        if v := due(pe, xin_ready, t, 4):
                                            pe.wait_ge(xin_ready.sem, v)
                                        for et in (2 * p, 2 * p + 1):
                                            last = matmul(work[2][0:N, 0:T], wb[:, et, :], x[:, et, :],
                                                          start=(et == 0), stop=(et == ET - 1))
                                    if s == 26 + p:
                                        if v := due(pe, low_ready, t, 1):
                                            pe.wait_ge(low_ready.sem, v)
                                        if p % 2 and (v := due(pe, c_ready, t, 1)):
                                            pe.wait_ge(c_ready.sem, v)
                                        if v := due(pe, z_read, t, p - 1):
                                            pe.wait_ge(z_read.sem, v)
                                        for e in range(2):
                                            et = 2 * p + e
                                            last = matmul(pair_bank(p)[:, e * T:(e + 1) * T],
                                                          wd2[:, et * P:(et + 1) * P], low[:], start=True, stop=True)
                                        last.then_inc(z_done.sem, 1)
                                    if s == (25, 27, 29, 30)[p]:
                                        bank = work[(3, 3, 0, 3)[p]]
                                        if v := due(pe, xd_ready, t, p + 1):
                                            pe.wait_ge(xd_ready.sem, v)
                                        if v := due(pe, o_ready, t, TB):
                                            pe.wait_ge(o_ready.sem, v)
                                        if p == 2 and (v := due(pe, z_ready, t, TB)):
                                            pe.wait_ge(z_ready.sem, v)
                                        if p % 2 and (v := due(pe, acc_init, t, (0, 1, 0, 2)[p])):
                                            pe.wait_ge(acc_init.sem, v)
                                        if v := due(pe, acc_init, t - 1, PAIRS):
                                            pe.wait_ge(acc_init.sem, v)
                                        for b in range(TB):
                                            for e in range(2):
                                                last = transpose(bank[:, (2 * b + e) * P:(2 * b + e + 1) * P],
                                                                 hv[:, p % 2, e, b * P:(b + 1) * P], ident[:])
                                        last.then_inc(xd_turned.sem, 1)
                                if s == 25:
                                    for b in range(TB):
                                        for et in range(ET):
                                            last = matmul(work[2][:, T + b * N:T + (b + 1) * N],
                                                          x[:, et, b * P:(b + 1) * P], wc[:, et, :],
                                                          start=(et == 0), stop=(et == ET - 1))
                                    last.then_inc(c_done.sem, 1)
                            if "mix" in jobs_now:
                                for p in range(PAIRS):
                                    if s in (2 * p, 2 * p + 1):
                                        e = s % 2
                                        if v := due(pe, z_read, t - 1, min(3 + p, PAIRS)):
                                            pe.wait_ge(z_read.sem, v)
                                        if v := due(pe, gate_ready, t, p - 1):
                                            pe.wait_ge(gate_ready.sem, v)
                                        for k in range(KD):
                                            last = matmul(pair_bank(p)[:, e * T:(e + 1) * T],
                                                          wskip[:, k, (2 * p + e) * P:(2 * p + e + 1) * P],
                                                          rnt[:, other, k, :], start=(k == 0), stop=(k == KD - 1))
                                        if e == 1:
                                            last.then_inc(skip_done.sem, 1)
                                    if s == 2 * p + 3:
                                        if v := due(pe, y_added, t - 1, SLOTS * TB):
                                            pe.wait_ge(y_added.sem, v)
                                        if v := due(pe, acc_init, t - 1, 3):
                                            pe.wait_ge(acc_init.sem, v)
                                        if v := due(pe, z_ready, t - 1, TB):
                                            pe.wait_ge(z_ready.sem, v)
                                        if p and (v := due(pe, ys_ready, t, p)):
                                            pe.wait_ge(ys_ready.sem, v)
                                        for e in range(2):
                                            for b in range(TB):
                                                last = transpose(work[0][:, (2 * e + b) * P:(2 * e + b + 1) * P],
                                                                 acc[:, other, b, (2 * p + e) * P:(2 * p + e + 1) * P],
                                                                 ident[:])
                                        last.then_inc(y_turned.sem, 1)
                                if 11 <= s < 11 + ET or 20 <= s < 20 + ET:
                                    b = int(s >= 20)
                                    et = s - (11, 20)[b]
                                    if v := due(pe, ys_ready, t, PAIRS):
                                        pe.wait_ge(ys_ready.sem, v)
                                    if b and (v := due(pe, z_ready, t, b)):
                                        pe.wait_ge(z_ready.sem, v)
                                    last = matmul(work[0][:], ys[:, et, b * P:(b + 1) * P], wout[:, et, :],
                                                  start=(et == 0), stop=(et == ET - 1))
                                    if et == ET - 1:
                                        last.then_inc(out_done.sem, 1)
                            if "route" in jobs_now:
                                if s in (10, 12):
                                    b = (s - 10) // 2
                                    if v := due(pe, h2_ready, t, b + 1):
                                        pe.wait_ge(h2_ready.sem, v)
                                    if v := due(pe, acc_init, t - 1, PAIRS):
                                        pe.wait_ge(acc_init.sem, v)
                                    if b and (v := due(pe, h2t_ready, t, b)):
                                        pe.wait_ge(h2t_ready.sem, v)
                                    if v := due(pe, o_ready, t - 1, TB):
                                        pe.wait_ge(o_ready.sem, v)
                                    for k in range(KD):
                                        last = transpose(work[3][:, k * P:(k + 1) * P],
                                                         h2[:, b, k * P:(k + 1) * P], ident[:])
                                    last.then_inc(h2_turned.sem, 1)
                                if s == 14:
                                    if v := due(pe, h2t_ready, t, TB):
                                        pe.wait_ge(h2t_ready.sem, v)
                                    for b in range(TB):
                                        logits = work[3][:, b * EXPERTS:(b + 1) * EXPERTS]
                                        for k in range(KD):
                                            matmul(logits, h2t[:, b, k, :], wrouter[:, k, :], start=(k == 0),
                                                   stop=False)
                                        last = matmul(logits, ones[:], rbias[:], start=False, stop=True)
                                    last.then_inc(logits_done.sem, 1)
                                if s == 19:
                                    if v := due(pe, w_ready, t, 1):
                                        pe.wait_ge(w_ready.sem, v)
                                    for b in range(TB):
                                        last = transpose(work[3][0:EXPERTS, b * P:(b + 1) * P], ex[:, b], ident[:])
                                    last.then_inc(w_turned.sem, 1)
                                if s in (21, 23):
                                    b = (s - 21) // 2
                                    if v := due(pe, wt_ready, t, 1):
                                        pe.wait_ge(wt_ready.sem, v)
                                    if b and (v := due(pe, o_ready, t, b)):
                                        pe.wait_ge(o_ready.sem, v)
                                    matmul(work[3][:], wt[:, b], ebias[:], start=True,
                                           stop=True).then_inc(eb_done.sem, 1)
            clear_semaphores()

        everything = ("prep", "scan", "mix", "route")
        section(-1, [("prep",), ("prep", "scan"), ("prep", "scan", "mix")], 1)
        with nc.Fori(0, (CHUNKS - 4) // 2) as pair:
            section(pair * 2 + 2, [everything, everything], 0)
        section(CHUNKS - 2, [everything, ("scan", "mix", "route"), ("mix", "route"), ("route",)], 0)


_INS = ['L0_attn_resid', 'L0_attn_norm_w', 'L0_attn_W_skip', 'L0_attn_W_in', 'L0_attn_conv_w', 'L0_attn_conv_b',
        'L0_attn_W_delta_1', 'L0_attn_W_delta_2', 'L0_attn_b_delta_2', 'L0_attn_W_B', 'L0_attn_W_C', 'L0_attn_A_log',
        'L0_attn_W_D', 'L0_attn_W_out', 'L0_ffn_router_weight', 'L0_ffn_router_bias', 'L0_ffn_expert_bias']


def kernel(**inputs):
    import numpy as _np
    import concourse.bacc as _bacc
    from concourse import mybir as _mybir
    from concourse.bass_utils import run_bass_kernel_spmd as _run

    nc = _bacc.Bacc("TRN2", target_bir_lowering=False, num_devices=1)
    arrays, args = {}, []
    for name in _INS:
        a = _np.ascontiguousarray(inputs[name])
        arrays[f"in_{name}"] = a
        args.append(nc.dram_tensor(f"in_{name}", a.shape, _mybir.dt.from_np(a.dtype), kind="ExternalInput").ap())
    shape = arrays["in_L0_attn_resid"].shape
    args.append(nc.dram_tensor("out_0", shape, _mybir.dt.float32, kind="ExternalOutput").ap())
    build(nc, *args)
    r = _run(nc, [arrays], core_ids=[0])
    return r.results[0]["out_0"]
```

```python
import concourse.bass as bass
from concourse import mybir
from contextlib import ExitStack

P = 128
D = 512
E = 1024
N = 16
DELTA = 128
TAPS = 4
EXPERTS = 64
TOP = 8
BATCH, LEN = 2, 2048
EPS = 1e-5
T = 256
CHUNKS = BATCH * LEN // T
PER_BATCH = LEN // T
TB = T // P
KD = D // P
ET = E // P
HALF = ET // 2
PAIRS = ET // 2
BANKS = HALF // 2
SLOTS = 2 * N
GROUP = 4


class Signal:

    def __init__(self, nc, stack, name, job, per, unit=1):
        self.sem = stack.enter_context(nc.semaphore(name))
        self.job, self.per, self.unit = job, per, unit


class Section:

    def __init__(self, first, jobs):
        self.first, self.jobs, self.seen = first, jobs, {}

    def value(self, signal, step, event):
        while event <= 0:
            step, event = step - 1, event + signal.per
        if step < 0 or signal.job not in self.jobs[step]:
            return 0
        before = sum(signal.job in jobs for jobs in self.jobs[:step])
        return (before * signal.per + event) * signal.unit

    def due(self, engine, signal, step, event):
        value = self.value(signal, step, event)
        key = id(engine), signal.sem.num
        if value <= self.seen.get(key, 0):
            return 0
        self.seen[key] = value
        return value


class Chain:

    def __init__(self, nc, stack, name):
        self.sem, self.count = stack.enter_context(nc.semaphore(name)), 0

    def link(self, engine, instruction):
        self.count += 1
        instruction.then_inc(self.sem, 1)
        engine.wait_ge(self.sem, self.count)


def build(nc, resid, norm_w, w_skip, w_in, conv_w, conv_b, w_delta_1, w_delta_2, b_delta_2, w_b, w_c, a_log,
          w_d, w_out, router_w, router_b, expert_b, out):
    F32 = mybir.dt.float32
    ALU, ACT, AX = mybir.AluOpType, mybir.ActivationFunctionType, mybir.AxisListType
    x_rows = resid.rearrange("b l d -> (b l) d")
    out_rows = out.rearrange("b l d -> (b l) d")
    b_rows = nc.dram_tensor("b_rows", [2, N, T], F32).ap()

    with ExitStack() as stack:
        def sb(name, *shape):
            return stack.enter_context(nc.sbuf_tensor(name, list(shape), F32))

        win, wskip = sb("win", P, KD, E), sb("wskip", P, KD, E)
        wout = sb("wout", P, ET, D)
        wd1, wd2 = sb("wd1", P, ET, DELTA), sb("wd2", P, E)
        wb, wc = sb("wb", P, ET, N), sb("wc", P, ET, N)
        wrouter, ebias = sb("wrouter", P, KD, EXPERTS), sb("ebias", EXPERTS, D)
        neg_a = sb("neg_a", P, ET, N)
        taps, cbias = sb("taps", P, ET, TAPS), sb("cbias", P, ET)
        bdelta, dskip, nw = sb("bdelta", P, ET), sb("dskip", P, ET), sb("nw", P, KD)
        rbias, ones = sb("rbias", 1, EXPERTS), sb("ones", 1, P)
        ident, mhalf = sb("ident", P, P), sb("mhalf", P, TB)
        keep = sb("keep", P, CHUNKS + 2)
        xn = sb("xn", P, TB, D)
        rnt, rnt_gate = sb("rnt", P, KD, T), sb("rnt_gate", P, KD, T)
        kept, kept_now = sb("kept", P, 2, 4, TB), sb("kept_now", P, 4, TB)
        xin = sb("xin", P, 2, 2, T + TAPS)
        halo = sb("halo", P, ET, TAPS - 1)
        hv = sb("hv", P, 2, 2, T)
        th = sb("th", P, 2, 2, T)
        x = sb("x", P, ET, T)
        low = sb("low", P, T)
        delta, dx = sb("delta", P, 2, ET, T), sb("dx", P, 2, ET, T)
        b_sb, c_t = sb("b_sb", N, T), sb("c_t", P, 2, TB, N)
        b_all = sb("b_all", P, 2, GROUP, T)
        u, h = sb("u", P, 2, HALF, T), sb("h", P, 2, HALF, T)
        carry = sb("carry", P, N, ET)
        first_decay, first_state = sb("first_decay", P, N, ET // 2), sb("first_state", P, N, ET // 2)
        acc = sb("acc", P, 2, TB, E)
        thg, gate = sb("thg", P, 2, 2, T), sb("gate", P, 2, 2, T)
        ys = sb("ys", P, ET, T)
        xp, z = sb("xp", P, TB, D), sb("z", P, TB, D)
        x1, h2 = sb("x1", P, TB, D), sb("h2", P, TB, D)
        o = gate[:].rearrange("p s e t -> p s (e t)")
        h2t = thg[:].rearrange("p s e (k t) -> p s (e k) t", t=P)
        ex, rem, wt = sb("ex", P, TB, EXPERTS), sb("rem", P, TB, EXPERTS), sb("wt", EXPERTS, TB, P)
        top8 = sb("top8", P, TB, TOP)
        stat6 = sb("stat6", P, TB, 6)
        mvx, mvz, mvh, mvo = (sb(f"mv{n}", P, TB, 2) for n in "xzho")
        small = {n: sb(f"s_{n}", P, TB) for n in
                 ("varx", "r1", "ms", "r2", "s", "ns", "varz", "rz", "nz", "varh", "rh", "nh", "nmx", "se", "rs",
                  "ts", "varo", "ro", "no")}

        da = stack.enter_context(nc.psum_tensor("da", [P, 2, 2, T], F32))
        ht = stack.enter_context(nc.psum_tensor("ht", [P, TB, D], F32))
        work = [stack.enter_context(nc.psum_tensor(f"work{n}", [P, 512], F32)) for n in range(4)]

        signals = []

        def signal(name, job, per, unit=1):
            signals.append(Signal(nc, stack, name, job, per, unit))
            return signals[-1]

        exp_ready = signal("exp_ready", "scan", SLOTS * HALF)
        u_ready = signal("u_ready", "scan", SLOTS)
        scan_done = signal("scan_done", "scan", SLOTS * BANKS)
        carry_saved = signal("carry_saved", "scan", SLOTS)
        decay_ready = signal("decay_ready", "prep", 1)
        early_states, late_states = signal("early_states", "prep", 1), signal("late_states", "scan", 1)
        ht_ready = signal("ht_ready", "scan", SLOTS * TB)
        y_added = signal("y_added", "scan", SLOTS * TB)
        b_loaded = [signal(f"b_loaded{g}", "prep" if g < 2 else "scan", 1, 16) for g in range(N // GROUP)]
        xt_loaded, kept_moved = signal("xt_loaded", "scan", 1, 16), signal("kept_moved", "scan", 1)
        xt_normed = signal("xt_normed", "scan", TB)
        xt_turned, gate_rnt_ready = signal("xt_turned", "scan", 2), signal("gate_rnt_ready", "scan", 2)
        x_loaded = signal("x_loaded", "norm", 1, 16)
        var_x, r1_ready, ms_ready, r2_ready, s_ready = (
            signal(n, "norm", 1) for n in ("var_x", "r1_ready", "ms_ready", "r2_ready", "s_ready"))
        rn_ready = signal("rn_ready", "norm", TB)
        rn_turned, rnt_ready = signal("rn_turned", "norm", 2), signal("rnt_ready", "norm", 2)
        in_done, xin_ready = signal("in_done", "prep", PAIRS), signal("xin_ready", "prep", PAIRS)
        conv_done, halo_saved = signal("conv_done", "prep", PAIRS), signal("halo_saved", "prep", PAIRS)
        th_ready, x_ready = signal("th_ready", "prep", PAIRS), signal("x_ready", "prep", PAIRS)
        low_done, low_ready = signal("low_done", "prep", 1), signal("low_ready", "prep", 1)
        b_ready = signal("b_ready", "prep", 1)
        b_stored = signal("b_stored", "prep", 1, 16)
        c_done, c_ready = signal("c_done", "prep", 1), signal("c_ready", "prep", 1)
        z_done, z_read = signal("zd_done", "prep", PAIRS), signal("zd_read", "prep", PAIRS)
        exp_z, ln_ready = signal("exp_z", "prep", 2), signal("ln_ready", "prep", 2)
        delta_ready, dx_ready = signal("delta_ready", "prep", 2), signal("dx_ready", "prep", 2)
        xd_ready, xd_turned = signal("xd_ready", "prep", PAIRS), signal("xd_turned", "prep", PAIRS)
        acc_init = signal("acc_init", "prep", PAIRS)
        skip_done, thg_ready = signal("skip_done", "mix", PAIRS), signal("thg_ready", "mix", PAIRS)
        gate_ready = signal("gate_ready", "mix", PAIRS)
        y_turned, ys_ready = signal("y_turned", "mix", PAIRS), signal("ys_ready", "mix", PAIRS)
        xp_loaded, z0_ready = signal("xp_loaded", "mix", 1, 16), signal("z0_ready", "mix", TB)
        out_done, z_ready = signal("out_done", "mix", TB), signal("z_ready", "mix", TB)
        var_z, rz_ready, nz_ready, x1_ready = (
            signal(n, "route", 1) for n in ("var_z", "rz_ready", "nz_ready", "x1_ready"))
        var_h, rh_ready, nh_ready = (signal(n, "route", 1) for n in ("var_h", "rh_ready", "nh_ready"))
        zn_ready, h2_ready = signal("zn_ready", "route", TB), signal("h2_ready", "route", TB)
        h2_turned, h2t_ready = signal("h2_turned", "route", TB), signal("h2t_ready", "route", TB)
        logits_done, nmx_ready = signal("logits_done", "route", 1), signal("nmx_ready", "route", 1)
        e_ready, w_ready = signal("e_ready", "route", TB), signal("w_ready", "route", 1)
        w_turned, wt_ready = signal("w_turned", "route", 1), signal("wt_ready", "route", 1)
        eb_done, o_ready = signal("eb_done", "route", TB), signal("o_ready", "route", TB)
        var_o, ro_ready, no_ready = (signal(n, "route", 1) for n in ("var_o", "ro_ready", "no_ready"))
        on_ready, out_ready = signal("on_ready", "route", TB), signal("out_ready", "route", 1)
        out_stored = signal("out_stored", "route", 1, 16)
        dve_chain, pool_chain = Chain(nc, stack, "dve_chain"), Chain(nc, stack, "pool_chain")
        loads = stack.enter_context(nc.semaphore("loads"))
        a_ready, ident_made = stack.enter_context(nc.semaphore("a_ready")), stack.enter_context(nc.semaphore("ident_made"))
        router_in, router_turned, vectors_ready = (
            stack.enter_context(nc.semaphore(n)) for n in ("router_in", "router_turned", "vectors_ready"))
        numbers = [s.sem.num for s in signals] + [s.num for s in
                   (dve_chain.sem, pool_chain.sem, loads, a_ready, ident_made, router_in, router_turned, vectors_ready)]

        def clear_semaphores():
            nc.sync.sem_clear(range(min(numbers), max(numbers) + 1))
            nc.all_engine_barrier(sem_only=True)

        with nc.Block() as block:
            tiles = lambda w: w.rearrange("(k p) n -> p k n", p=P)
            router_rows = x1[0:EXPERTS, 0, :]
            vector_rows = h2[0:KD + (TAPS + 3) * ET, 0, 0:P]
            vectors = [norm_w, conv_b, b_delta_2, w_d] + [conv_w[k, 0] for k in range(TAPS)]
            small_loads, row = [(router_rows, router_w)], 0
            for v in vectors:
                rows_of_v = v.rearrange("(k p) -> k p", p=P)
                small_loads.append((vector_rows[row:row + rows_of_v.shape[0], :], rows_of_v))
                row += rows_of_v.shape[0]
            small_loads += [(neg_a[:], tiles(a_log)), (rbias[:], router_b.unsqueeze(0)), (ebias[:], expert_b),
                            (wb[:], tiles(w_b)), (wc[:], tiles(w_c))]
            large_loads = [(win[:], tiles(w_in)), (wskip[:], tiles(w_skip)), (wout[:], tiles(w_out)),
                           (wd1[:], tiles(w_delta_1)), (wd2[:], w_delta_2)]

            @block.sync
            def _(sp):
                for to, of in small_loads:
                    sp.dma_start(to, of).then_inc(router_in, 16)
                for to, of in large_loads:
                    sp.dma_start(to, of).then_inc(loads, 16)
                sp.wait_ge(router_in, 16 * len(small_loads))
                sp.wait_ge(loads, 16 * len(large_loads))

            @block.gpsimd
            def _(pool):
                nc.gpsimd.memset(ident[:], 0.0).then_inc(ident_made, 1)
                pool.wait_ge(ident_made, 1)
                nc.gpsimd.affine_select(out=ident[:], in_=ident[:], compare_op=ALU.not_equal, fill=1.0, base=0,
                                        pattern=[[-1, P]], channel_multiplier=1).then_inc(ident_made, 1)
                nc.gpsimd.memset(mhalf[:], -0.5)
                nc.gpsimd.memset(ones[:], 1.0)
                nc.gpsimd.memset(carry[:], 0.0)
                nc.gpsimd.memset(halo[:], 0.0)

            @block.scalar
            def _(act):
                act.wait_ge(router_in, 16 * len(small_loads))
                nc.scalar.activation(neg_a[:], neg_a[:], ACT.Exp).then_inc(a_ready, 1)
                act.wait_ge(router_turned, 1)
                nc.scalar.activation(wrouter[:].rearrange("p k e -> p (k e)"), work[0][:, 0:KD * EXPERTS], ACT.Copy)
                turned, at = work[1], 0
                for to, scale in ((nw[:], 1.0), (cbias[:], 0.5), (bdelta[:], 1.0), (dskip[:], 1.0)):
                    nc.scalar.activation(to, turned[:, at:at + to.shape[1]], ACT.Copy,
                                         scale=scale).then_inc(vectors_ready, 1)
                    at += to.shape[1]
                nc.scalar.activation(taps[:], turned[:, at:at + TAPS * ET].rearrange("p (k e) -> p e k", k=TAPS),
                                     ACT.Copy, scale=0.5)
                act.wait_ge(vectors_ready, 1)
                act.wait_ge(loads, 16 * len(large_loads))
                for k in range(KD):
                    nc.scalar.activation(wskip[:, k, :], wskip[:, k, :], ACT.Copy, scale=nw[:, k:k + 1])

            @block.vector
            def _(dve):
                dve_chain.link(dve, nc.vector.memset(keep[:], 1.0))
                nc.vector.memset(da[:, :, 1, 0:1], 0.0)
                dve.wait_ge(router_in, 16 * len(small_loads))
                for j in range(0, CHUNKS + 2, PER_BATCH):
                    dve_chain.link(dve, nc.vector.memset(keep[:, j:j + 1], 0.0))
                dve.wait_ge(a_ready, 1)
                nc.vector.tensor_scalar(neg_a[:], neg_a[:], -1.0, None, ALU.mult)
                dve.wait_ge(loads, 16 * len(large_loads))
                dve.wait_ge(vectors_ready, 1)
                nc.vector.tensor_scalar(wout[:], wout[:], 0.5, None, ALU.mult)
                for k in range(KD):
                    nc.vector.tensor_scalar(win[:, k, :], win[:, k, :], nw[:, k:k + 1], None, ALU.mult)

            @block.tensor
            def _(pe):
                pe.wait_ge(router_in, 16 * len(small_loads))
                pe.wait_ge(ident_made, 2)
                for k in range(KD):
                    nc.tensor.transpose(work[0][:, k * EXPERTS:(k + 1) * EXPERTS],
                                               router_rows[:, k * P:(k + 1) * P], ident[0:EXPERTS, 0:EXPERTS])
                nc.tensor.transpose(work[1][:, 0:vector_rows.shape[0]], vector_rows,
                                    ident[0:vector_rows.shape[0], 0:vector_rows.shape[0]]).then_inc(router_turned, 1)
        clear_semaphores()

        def pair_bank(p):
            return work[1 + p % 2]

        def section(first, jobs, parity):
            sec = Section(first, jobs)
            dve_chain.count = pool_chain.count = 0
            due = sec.due

            def rows(chunk):
                return bass.ds(chunk * T, T)

            def per_block(ap):
                return ap.rearrange("(b p) d -> p b d", p=P)

            with nc.Block() as block:
                @block.sync
                def _(sp):
                    def load_b(side, group):
                        src = b_rows[side, group * GROUP:(group + 1) * GROUP].unsqueeze(0)
                        sp.dma_start(b_all[:, group % 2], src.to_broadcast([P, GROUP, T])).then_inc(
                            b_loaded[group].sem, 16)

                    for t, jobs_now in enumerate(jobs):
                        i, now = first + t, (parity + t) % 2
                        for s in range(SLOTS):
                            if "norm" in jobs_now and s == 13:
                                if v := due(sp, rn_turned, t - 1, 2):
                                    sp.wait_ge(rn_turned.sem, v)
                                sp.dma_start(xn[:], per_block(x_rows[rows(i + 2), :])).then_inc(x_loaded.sem, 16)
                            if "scan" in jobs_now and s == 26:
                                if v := due(sp, o_ready, t, TB):
                                    sp.wait_ge(o_ready.sem, v)
                                if v := due(sp, h2_turned, t, TB):
                                    sp.wait_ge(h2_turned.sem, v)
                                if v := due(sp, xt_turned, t - 1, 2):
                                    sp.wait_ge(xt_turned.sem, v)
                                sp.dma_start(h2[:], per_block(x_rows[rows(i), :])).then_inc(xt_loaded.sem, 16)
                            if "mix" in jobs_now and s == 8:
                                if v := due(sp, x1_ready, t, 1):
                                    sp.wait_ge(x1_ready.sem, v)
                                sp.dma_start(xp[:], per_block(x_rows[rows(i - 1), :])).then_inc(xp_loaded.sem, 16)
                            if "scan" in jobs_now and s in (8, 16):
                                group = 1 + s // 8
                                if v := due(sp, u_ready, t, (group - 1) * 2 * GROUP):
                                    sp.wait_ge(u_ready.sem, v)
                                load_b(now, group)
                            if "prep" in jobs_now and s == 19:
                                if v := due(sp, b_ready, t, 1):
                                    sp.wait_ge(b_ready.sem, v)
                                for done in b_loaded:
                                    if v := due(sp, done, t - 1 if done.job == "scan" else t - 2, 1):
                                        sp.wait_ge(done.sem, v)
                                sp.dma_start(b_rows[1 - now], b_sb[:]).then_inc(b_stored.sem, 16)
                            if "prep" in jobs_now and s == 28:
                                if v := due(sp, b_stored, t, 1):
                                    sp.wait_ge(b_stored.sem, v)
                                if v := due(sp, u_ready, t, 3 * 2 * GROUP):
                                    sp.wait_ge(u_ready.sem, v)
                                load_b(1 - now, 0)
                            if "route" in jobs_now and s == 30:
                                if v := due(sp, out_ready, t, 1):
                                    sp.wait_ge(out_ready.sem, v)
                                sp.dma_start(per_block(out_rows[rows(i - 2), :]), o).then_inc(out_stored.sem, 16)
                        if "prep" in jobs_now:
                            if v := due(sp, u_ready, t, SLOTS):
                                sp.wait_ge(u_ready.sem, v)
                            load_b(1 - now, 1)
                    for done in (x_loaded, xt_loaded, xp_loaded, *b_loaded, b_stored, out_stored):
                        for t in range(len(jobs)):
                            if v := due(sp, done, t, done.per):
                                sp.wait_ge(done.sem, v)

                @block.gpsimd
                def _(pool):
                    def rstd(to, var):
                        return nc.gpsimd.tensor_tensor(small[to][:], small[var][:], mhalf[:], ALU.pow)

                    def drive(t, s):
                        t, s = t + s // SLOTS, s % SLOTS
                        if t == len(jobs) or "scan" not in jobs[t]:
                            return
                        side = (parity + t) % 2
                        n, eh = s // 2, s % 2
                        group = n // GROUP
                        if v := due(pool, scan_done, t, BANKS * (s - 1)):
                            pool.wait_ge(scan_done.sem, v)
                        if v := due(pool, b_loaded[group], t - 1 if group < 2 else t, 1):
                            pool.wait_ge(b_loaded[group].sem, v)
                        if v := due(pool, dx_ready, t - 1, eh + 1):
                            pool.wait_ge(dx_ready.sem, v)
                        b_row = b_all[:, group % 2, n % GROUP:n % GROUP + 1, :]
                        pool_chain.link(pool, nc.gpsimd.tensor_tensor(
                            u[:, s % 2], dx[:, side, eh * HALF:(eh + 1) * HALF, :],
                            b_row.to_broadcast([P, HALF, T]), ALU.mult))
                        states, step = (early_states, t - 1) if s < SLOTS // 2 else (late_states, t)
                        if v := due(pool, states, step, 1):
                            pool.wait_ge(states.sem, v)
                        starts = u[:, s % 2, 1::2, 0]
                        nc.gpsimd.tensor_tensor(starts, starts, first_state[:, n, eh * BANKS:(eh + 1) * BANKS],
                                                ALU.add).then_inc(u_ready.sem, 1)

                    drive(0, 0)
                    for t, jobs_now in enumerate(jobs):
                        now, other = (parity + t) % 2, (parity + t + 1) % 2
                        for s in range(SLOTS):
                            drive(t, s + 1)
                            if "scan" in jobs_now and s == 2:
                                if v := due(pool, decay_ready, t - 1, 1):
                                    pool.wait_ge(decay_ready.sem, v)
                                if v := due(pool, carry_saved, t - 1, SLOTS):
                                    pool.wait_ge(carry_saved.sem, v)
                                nc.gpsimd.tensor_tensor(first_state[:, N // 2:], first_decay[:, N // 2:],
                                                        carry[:, N // 2:, 1::2],
                                                        ALU.mult).then_inc(late_states.sem, 1)
                            if "prep" in jobs_now and s == 30:
                                if v := due(pool, decay_ready, t, 1):
                                    pool.wait_ge(decay_ready.sem, v)
                                if v := due(pool, carry_saved, t, SLOTS // 2):
                                    pool.wait_ge(carry_saved.sem, v)
                                nc.gpsimd.tensor_tensor(first_state[:, :N // 2], first_decay[:, :N // 2],
                                                        carry[:, :N // 2, 1::2],
                                                        ALU.mult).then_inc(early_states.sem, 1)
                            if "norm" in jobs_now:
                                if s == 16:
                                    if v := due(pool, var_x, t, 1):
                                        pool.wait_ge(var_x.sem, v)
                                    rstd("r1", "varx").then_inc(r1_ready.sem, 1)
                                if s == 18:
                                    if v := due(pool, ms_ready, t, 1):
                                        pool.wait_ge(ms_ready.sem, v)
                                    rstd("r2", "ms").then_inc(r2_ready.sem, 1)
                            if "prep" in jobs_now:
                                for eh in range(2):
                                    if s == 26 + 2 * eh:
                                        part = slice(eh * HALF, (eh + 1) * HALF)
                                        if v := due(pool, delta_ready, t, eh + 1):
                                            pool.wait_ge(delta_ready.sem, v)
                                        nc.gpsimd.tensor_tensor(dx[:, other, part], delta[:, other, part], x[:, part],
                                                                ALU.mult).then_inc(dx_ready.sem, 1)
                            if "route" in jobs_now:
                                if s == 1:
                                    if v := due(pool, var_z, t, 1):
                                        pool.wait_ge(var_z.sem, v)
                                    rstd("rz", "varz").then_inc(rz_ready.sem, 1)
                                if s == 4:
                                    if v := due(pool, zn_ready, t, TB):
                                        pool.wait_ge(zn_ready.sem, v)
                                    if v := due(pool, xp_loaded, t - 1, 1):
                                        pool.wait_ge(xp_loaded.sem, v)
                                    if v := due(pool, out_ready, t - 1, 1):
                                        pool.wait_ge(out_ready.sem, v)
                                    nc.gpsimd.tensor_tensor(x1[:], xp[:], z[:], ALU.add).then_inc(x1_ready.sem, 1)
                                if s == 7:
                                    if v := due(pool, var_h, t, 1):
                                        pool.wait_ge(var_h.sem, v)
                                    rstd("rh", "varh").then_inc(rh_ready.sem, 1)
                                if s == 26:
                                    if v := due(pool, var_o, t, 1):
                                        pool.wait_ge(var_o.sem, v)
                                    rstd("ro", "varo").then_inc(ro_ready.sem, 1)
                                if s == 29:
                                    if v := due(pool, on_ready, t, TB):
                                        pool.wait_ge(on_ready.sem, v)
                                    if v := due(pool, x1_ready, t, 1):
                                        pool.wait_ge(x1_ready.sem, v)
                                    nc.gpsimd.tensor_tensor(o, x1[:], o, ALU.add).then_inc(out_ready.sem, 1)

                @block.scalar
                def _(act):
                    def scaled(to, of, scale, bias):
                        return nc.scalar.activation(to, of, ACT.Identity, bias=bias, scale=scale)

                    def decay(t, s):
                        t, s = t + s // SLOTS, s % SLOTS
                        if t == len(jobs) or "scan" not in jobs[t]:
                            return
                        side = (parity + t) % 2
                        n, eh = s // 2, s % 2
                        if v := due(act, delta_ready, t - 1, eh + 1):
                            act.wait_ge(delta_ready.sem, v)
                        for q in range(HALF):
                            et = eh * HALF + q
                            if v := due(act, scan_done, t, BANKS * (s - 1) + q // 2 + 1):
                                act.wait_ge(scan_done.sem, v)
                            nc.scalar.activation(da[:, q // 2, q % 2, q % 2:], delta[:, side, et, q % 2:], ACT.Exp,
                                                 scale=neg_a[:, et, n:n + 1]).then_inc(exp_ready.sem, 1)

                    decay(0, 0)
                    for t, jobs_now in enumerate(jobs):
                        now, other = (parity + t) % 2, (parity + t + 1) % 2
                        for s in range(SLOTS):
                            decay(t, s + 1)
                            if "scan" in jobs_now:
                                if s == 28:
                                    if v := due(act, xt_loaded, t, 1):
                                        act.wait_ge(xt_loaded.sem, v)
                                    if v := due(act, kept_moved, t, 1):
                                        act.wait_ge(kept_moved.sem, v)
                                    for b in range(TB):
                                        scaled(h2[:, b], h2[:, b], kept_now[:, 0, b:b + 1],
                                               kept_now[:, 1, b:b + 1]).then_inc(xt_normed.sem, 1)
                                if s in (30, 31):
                                    k = 2 * (s - 30)
                                    if v := due(act, xt_turned, t, k // 2 + 1):
                                        act.wait_ge(xt_turned.sem, v)
                                    if v := due(act, skip_done, t, PAIRS):
                                        act.wait_ge(skip_done.sem, v)
                                    nc.scalar.activation(rnt_gate[:, k:k + 2, :].rearrange("p k t -> p (k t)"),
                                                         work[3][:], ACT.Copy).then_inc(gate_rnt_ready.sem, 1)
                            if "norm" in jobs_now:
                                if s == 20:
                                    if v := due(act, s_ready, t, 1):
                                        act.wait_ge(s_ready.sem, v)
                                    for b in range(TB):
                                        scaled(xn[:, b], xn[:, b], kept[:, now, 0, b:b + 1],
                                               kept[:, now, 1, b:b + 1]).then_inc(rn_ready.sem, 1)
                                if s in (29, 30):
                                    k = 2 * (s - 29)
                                    if v := due(act, rn_turned, t, k // 2 + 1):
                                        act.wait_ge(rn_turned.sem, v)
                                    if v := due(act, in_done, t, PAIRS):
                                        act.wait_ge(in_done.sem, v)
                                    nc.scalar.activation(rnt[:, k:k + 2, :].rearrange("p k t -> p (k t)"),
                                                         pair_bank(k // 2)[:], ACT.Copy).then_inc(rnt_ready.sem, 1)
                            if "prep" in jobs_now:
                                for p in range(PAIRS):
                                    if s == 3 * p + 3:
                                        if v := due(act, in_done, t, p + 1):
                                            act.wait_ge(in_done.sem, v)
                                        if v := due(act, halo_saved, t, p - 1):
                                            act.wait_ge(halo_saved.sem, v)
                                        if v := due(act, x_ready, t, p - 1):
                                            act.wait_ge(x_ready.sem, v)
                                        if v := due(act, xd_turned, t - 1, PAIRS):
                                            act.wait_ge(xd_turned.sem, v)
                                        bank = pair_bank(p)[:].rearrange("p (e t) -> p e t", e=2)
                                        nc.scalar.activation(xin[:, p % 2, :, TAPS - 1:TAPS - 1 + T], bank, ACT.Copy)
                                        for e in range(2):
                                            et = 2 * p + e
                                            last = scaled(hv[:, p % 2, e, :], bank[:, e, :],
                                                          taps[:, et, TAPS - 1:TAPS], cbias[:, et:et + 1])
                                        last.then_inc(xin_ready.sem, 1)
                                    if s == 3 * p + 5:
                                        if v := due(act, conv_done, t, p + 1):
                                            act.wait_ge(conv_done.sem, v)
                                        if v := due(act, x_ready, t, p - 1):
                                            act.wait_ge(x_ready.sem, v)
                                        nc.scalar.activation(th[:, p % 2], hv[:, p % 2],
                                                             ACT.Tanh).then_inc(th_ready.sem, 1)
                                    if s == (16, 17, 25, 26)[p]:
                                        if v := due(act, x_ready, t, PAIRS):
                                            act.wait_ge(x_ready.sem, v)
                                        if v := due(act, xd_turned, t, p - 1):
                                            act.wait_ge(xd_turned.sem, v)
                                        for e in range(2):
                                            et = 2 * p + e
                                            last = nc.scalar.activation(hv[:, p % 2, e, :], x[:, et, :], ACT.Copy,
                                                                        scale=dskip[:, et:et + 1])
                                        last.then_inc(xd_ready.sem, 1)
                                    if s == (23, 25, 27, 28)[p]:
                                        if v := due(act, xd_turned, t, p + 1):
                                            act.wait_ge(xd_turned.sem, v)
                                        if v := due(act, y_turned, t, PAIRS):
                                            act.wait_ge(y_turned.sem, v)
                                        bank = pair_bank(p)[:].rearrange("p (b e) -> p b e", b=TB)
                                        nc.scalar.activation(acc[:, other, :, 2 * p * P:2 * (p + 1) * P], bank,
                                                             ACT.Copy).then_inc(acc_init.sem, 1)
                                    if s == 19 + p:
                                        if v := due(act, z_done, t, p + 1):
                                            act.wait_ge(z_done.sem, v)
                                        if v := due(act, exp_ready, t - 1, SLOTS * HALF):
                                            act.wait_ge(exp_ready.sem, v)
                                        if v := due(act, u_ready, t - 1, SLOTS):
                                            act.wait_ge(u_ready.sem, v)
                                        for e in range(2):
                                            et = 2 * p + e
                                            v = pair_bank(p)[:, e * T:(e + 1) * T]
                                            nc.scalar.activation(delta[:, other, et, :], v, ACT.Relu,
                                                                 bias=bdelta[:, et:et + 1])
                                            last = nc.scalar.activation(dx[:, other, et, :], v, ACT.Abs,
                                                                        bias=bdelta[:, et:et + 1])
                                        last.then_inc(z_read.sem, 1)
                                if s == 17:
                                    if v := due(act, low_done, t, 1):
                                        act.wait_ge(low_done.sem, v)
                                    if v := due(act, z_done, t - 1, PAIRS):
                                        act.wait_ge(z_done.sem, v)
                                    nc.scalar.activation(low[:], work[1][:, 0:T], ACT.Copy).then_inc(low_ready.sem, 1)
                                if s == 18:
                                    if v := due(act, c_done, t, 1):
                                        act.wait_ge(c_done.sem, v)
                                    if v := due(act, b_stored, t - 1, 1):
                                        act.wait_ge(b_stored.sem, v)
                                    nc.scalar.activation(b_sb[:], work[2][0:N, 0:T], ACT.Copy).then_inc(b_ready.sem, 1)
                                    if v := due(act, y_added, t - 1, SLOTS * TB):
                                        act.wait_ge(y_added.sem, v)
                                    nc.scalar.activation(c_t[:, other].rearrange("p b n -> p (b n)"),
                                                         work[2][:, T:T + TB * N], ACT.Copy).then_inc(c_ready.sem, 1)
                                if s == 29:
                                    if v := due(act, delta_ready, t, 2):
                                        act.wait_ge(delta_ready.sem, v)
                                    if v := due(act, late_states, t, 1):
                                        act.wait_ge(late_states.sem, v)
                                    for j in range(ET // 2):
                                        last = nc.scalar.activation(first_decay[:, :, j], neg_a[:, 2 * j + 1, :],
                                                                    ACT.Exp, scale=delta[:, other, 2 * j + 1, 0:1])
                                    last.then_inc(decay_ready.sem, 1)
                                if s == 23:
                                    if v := due(act, z_read, t, PAIRS):
                                        act.wait_ge(z_read.sem, v)
                                    for eh in range(2):
                                        part = dx[:, other, eh * HALF:(eh + 1) * HALF]
                                        nc.scalar.activation(part, part, ACT.Exp, scale=-1.0).then_inc(exp_z.sem, 1)
                                if s == 24:
                                    for eh in range(2):
                                        part = dx[:, other, eh * HALF:(eh + 1) * HALF]
                                        if v := due(act, exp_z, t, eh + 1):
                                            act.wait_ge(exp_z.sem, v)
                                        nc.scalar.activation(part, part, ACT.Ln, bias=1.0).then_inc(ln_ready.sem, 1)
                            if "mix" in jobs_now:
                                for p in range(PAIRS):
                                    if s == 3 * p + 1:
                                        if v := due(act, skip_done, t, p + 1):
                                            act.wait_ge(skip_done.sem, v)
                                        if v := due(act, gate_ready, t, p - 1):
                                            act.wait_ge(gate_ready.sem, v)
                                        if v := due(act, logits_done, t - 1, 1):
                                            act.wait_ge(logits_done.sem, v)
                                        nc.scalar.activation(thg[:, p % 2].rearrange("p e t -> p (e t)"),
                                                             work[3][:], ACT.Tanh,
                                                             scale=0.5).then_inc(thg_ready.sem, 1)
                                if s == 12:
                                    if v := due(act, xp_loaded, t, 1):
                                        act.wait_ge(xp_loaded.sem, v)
                                    if v := due(act, kept_moved, t - 1, 1):
                                        act.wait_ge(kept_moved.sem, v)
                                    if v := due(act, x1_ready, t, 1):
                                        act.wait_ge(x1_ready.sem, v)
                                    for b in range(TB):
                                        scaled(z[:, b], xp[:, b], kept_now[:, 2, b:b + 1],
                                               kept_now[:, 3, b:b + 1]).then_inc(z0_ready.sem, 1)
                            if "route" in jobs_now:
                                if s == 3:
                                    if v := due(act, nz_ready, t, 1):
                                        act.wait_ge(nz_ready.sem, v)
                                    for b in range(TB):
                                        scaled(z[:, b], z[:, b], small["rz"][:, b:b + 1],
                                               small["nz"][:, b:b + 1]).then_inc(zn_ready.sem, 1)
                                if s == 9:
                                    if v := due(act, nh_ready, t, 1):
                                        act.wait_ge(nh_ready.sem, v)
                                    if v := due(act, o_ready, t - 1, TB):
                                        act.wait_ge(o_ready.sem, v)
                                    if v := due(act, xt_turned, t - 1, 2):
                                        act.wait_ge(xt_turned.sem, v)
                                    for b in range(TB):
                                        scaled(h2[:, b], x1[:, b], small["rh"][:, b:b + 1],
                                               small["nh"][:, b:b + 1]).then_inc(h2_ready.sem, 1)
                                if s in (13, 15):
                                    b = (s - 13) // 2
                                    if v := due(act, h2_turned, t, b + 1):
                                        act.wait_ge(h2_turned.sem, v)
                                    if v := due(act, logits_done, t - 1, 1):
                                        act.wait_ge(logits_done.sem, v)
                                    if v := due(act, gate_ready, t, PAIRS):
                                        act.wait_ge(gate_ready.sem, v)
                                    nc.scalar.activation(h2t[:, b].rearrange("p k t -> p (k t)"), work[3][:],
                                                         ACT.Copy).then_inc(h2t_ready.sem, 1)
                                if s == 18:
                                    if v := due(act, nmx_ready, t, 1):
                                        act.wait_ge(nmx_ready.sem, v)
                                    if v := due(act, w_turned, t - 1, 1):
                                        act.wait_ge(w_turned.sem, v)
                                    for b in range(TB):
                                        nc.scalar.activation(ex[:, b], work[3][:, b * EXPERTS:(b + 1) * EXPERTS],
                                                             ACT.Exp, bias=small["nmx"][:, b:b + 1],
                                                             accum_out=small["se"][:, b:b + 1]).then_inc(e_ready.sem, 1)
                                if s == 21:
                                    if v := due(act, w_turned, t, 1):
                                        act.wait_ge(w_turned.sem, v)
                                    if v := due(act, eb_done, t - 1, TB):
                                        act.wait_ge(eb_done.sem, v)
                                    nc.scalar.activation(wt[:].rearrange("e b t -> e (b t)"),
                                                         work[3][0:EXPERTS, 0:TB * P],
                                                         ACT.Copy).then_inc(wt_ready.sem, 1)
                                if s == 28:
                                    if v := due(act, no_ready, t, 1):
                                        act.wait_ge(no_ready.sem, v)
                                    for b in range(TB):
                                        scaled(o[:, b], o[:, b], small["ro"][:, b:b + 1],
                                               small["no"][:, b:b + 1]).then_inc(on_ready.sem, 1)

                @block.vector
                def _(dve):
                    def link(instruction):
                        dve_chain.link(dve, instruction)

                    def moments(of, mv, var, ready):
                        for b in range(TB):
                            last = nc.vector.bn_stats(stat6[:, b], of[:, b])
                        link(last)
                        for b in range(TB):
                            last = nc.vector.bn_aggr(mv[:, b], stat6[:, b])
                        link(last)
                        nc.vector.tensor_scalar(small[var][:], mv[:, :, 1], EPS, None, ALU.add).then_inc(ready.sem, 1)

                    def minus_mean_times(to, mv, r):
                        return nc.vector.scalar_tensor_tensor(out=to, in0=mv[:, :, 0], scalar=-1.0, in1=r,
                                                              op0=ALU.mult, op1=ALU.mult)

                    def finish(t, s):
                        now, n, eh = (parity + t) % 2, s // 2, s % 2
                        if v := due(dve, scan_done, t, BANKS * (s + 1)):
                            dve.wait_ge(scan_done.sem, v)
                        states, step = (early_states, t - 1) if s < SLOTS // 2 else (late_states, t)
                        if v := due(dve, states, step, 1):
                            dve.wait_ge(states.sem, v)
                        nc.vector.tensor_tensor(carry[:, n, eh * HALF:(eh + 1) * HALF], h[:, s % 2, :, T - 1],
                                                keep[:, bass.ds(first + t + 1, 1)].to_broadcast([P, HALF]),
                                                ALU.mult).then_inc(carry_saved.sem, 1)
                        if v := due(dve, c_ready, t - 1, 1):
                            dve.wait_ge(c_ready.sem, v)
                        if v := due(dve, acc_init, t - 1, PAIRS):
                            dve.wait_ge(acc_init.sem, v)
                        for b in range(TB):
                            y = acc[:, now, b, eh * D:(eh + 1) * D]
                            if v := due(dve, ht_ready, t, TB * s + b + 1):
                                dve.wait_ge(ht_ready.sem, v)
                            if v := due(dve, y_added, t, TB * (s - 2) + b + 1):
                                dve.wait_ge(y_added.sem, v)
                            nc.vector.scalar_tensor_tensor(out=y, in0=ht[:, b], scalar=c_t[:, now, b, n:n + 1], in1=y,
                                                           op0=ALU.mult, op1=ALU.add).then_inc(y_added.sem, 1)

                    unfinished = None
                    for t, jobs_now in enumerate(jobs):
                        now, other = (parity + t) % 2, (parity + t + 1) % 2
                        for s in range(SLOTS):
                            if "scan" in jobs_now:
                                n, eh = s // 2, s % 2
                                if v := due(dve, u_ready, t, s + 1):
                                    dve.wait_ge(u_ready.sem, v)
                                if v := due(dve, ht_ready, t, TB * (s - 1)):
                                    dve.wait_ge(ht_ready.sem, v)
                                if v := due(dve, carry_saved, t, s - 1):
                                    dve.wait_ge(carry_saved.sem, v)
                                for q in range(0, HALF, 2):
                                    et = eh * HALF + q
                                    if v := due(dve, exp_ready, t, HALF * s + q + 2):
                                        dve.wait_ge(exp_ready.sem, v)
                                    nc.vector.tensor_tensor_scan(
                                        h[:, s % 2, q:q + 2, :].rearrange("p q t -> p (q t)"),
                                        da[:, q // 2].rearrange("p q t -> p (q t)"),
                                        u[:, s % 2, q:q + 2, :].rearrange("p q t -> p (q t)"),
                                        carry[:, n, et:et + 1], ALU.mult, ALU.add).then_inc(scan_done.sem, 1)
                                if unfinished:
                                    finish(*unfinished)
                                unfinished = t, s
                            elif unfinished:
                                finish(*unfinished)
                                unfinished = None
                            if "scan" in jobs_now and s == 14:
                                if v := due(dve, z0_ready, t, TB):
                                    dve.wait_ge(z0_ready.sem, v)
                                if v := due(dve, xt_normed, t - 1, TB):
                                    dve.wait_ge(xt_normed.sem, v)
                                if v := due(dve, s_ready, t - 2, 1):
                                    dve.wait_ge(s_ready.sem, v)
                                nc.vector.tensor_copy(kept_now[:], kept[:, now]).then_inc(kept_moved.sem, 1)
                            if "norm" in jobs_now:
                                if s == 15:
                                    if v := due(dve, x_loaded, t, 1):
                                        dve.wait_ge(x_loaded.sem, v)
                                    moments(xn, mvx, "varx", var_x)
                                if s == 17:
                                    if v := due(dve, r1_ready, t, 1):
                                        dve.wait_ge(r1_ready.sem, v)
                                    link(nc.vector.tensor_tensor(small["ms"][:], small["r1"][:], small["r1"][:],
                                                                 ALU.mult))
                                    link(nc.vector.tensor_tensor(small["ms"][:], small["ms"][:], mvx[:, :, 1],
                                                                 ALU.mult))
                                    nc.vector.tensor_scalar(small["ms"][:], small["ms"][:], EPS, None,
                                                            ALU.add).then_inc(ms_ready.sem, 1)
                                if s == 19:
                                    if v := due(dve, r2_ready, t, 1):
                                        dve.wait_ge(r2_ready.sem, v)
                                    if v := due(dve, kept_moved, t, 1):
                                        dve.wait_ge(kept_moved.sem, v)
                                    nc.vector.tensor_copy(kept[:, now, 2], small["r1"][:])
                                    minus_mean_times(kept[:, now, 3], mvx, small["r1"][:])
                                    link(nc.vector.tensor_tensor(kept[:, now, 0], small["r1"][:], small["r2"][:],
                                                                 ALU.mult))
                                    minus_mean_times(kept[:, now, 1], mvx,
                                                     kept[:, now, 0]).then_inc(s_ready.sem, 1)
                            if "prep" in jobs_now:
                                for p in range(PAIRS):
                                    if s == 3 * p + 4:
                                        xi = xin[:, p % 2]
                                        if v := due(dve, xin_ready, t, p + 1):
                                            dve.wait_ge(xin_ready.sem, v)
                                        if v := due(dve, halo_saved, t - 1, p + 1):
                                            dve.wait_ge(halo_saved.sem, v)
                                        link(nc.vector.tensor_copy(xi[:, :, 0:TAPS - 1], halo[:, 2 * p:2 * p + 2, :]))
                                        for k in range(TAPS - 1):
                                            for e in range(2):
                                                v = hv[:, p % 2, e, :]
                                                last = nc.vector.scalar_tensor_tensor(
                                                    out=v, in0=xi[:, e, k:k + T], scalar=taps[:, 2 * p + e, k:k + 1],
                                                    in1=v, op0=ALU.mult, op1=ALU.add)
                                            if k < TAPS - 2:
                                                link(last)
                                        last.then_inc(conv_done.sem, 1)
                                        nc.vector.tensor_tensor(
                                            halo[:, 2 * p:2 * p + 2, :], xi[:, :, T:T + TAPS - 1],
                                            keep[:, bass.ds(first + t + 2, 1)].unsqueeze(1)
                                            .to_broadcast([P, 2, TAPS - 1]), ALU.mult).then_inc(halo_saved.sem, 1)
                                    if s == 3 * p + 6:
                                        if v := due(dve, th_ready, t, p + 1):
                                            dve.wait_ge(th_ready.sem, v)
                                        if v := due(dve, dx_ready, t - 1, 2):
                                            dve.wait_ge(dx_ready.sem, v)
                                        if v := due(dve, c_done, t - 1, 1):
                                            dve.wait_ge(c_done.sem, v)
                                        if v := due(dve, xd_ready, t - 1, PAIRS):
                                            dve.wait_ge(xd_ready.sem, v)
                                        nc.vector.scalar_tensor_tensor(
                                            out=x[:, 2 * p:2 * p + 2, :], in0=th[:, p % 2], scalar=1.0,
                                            in1=hv[:, p % 2], op0=ALU.add, op1=ALU.mult).then_inc(x_ready.sem, 1)
                                for eh in range(2):
                                    if s == 25 + eh:
                                        part = slice(eh * HALF, (eh + 1) * HALF)
                                        if v := due(dve, ln_ready, t, eh + 1):
                                            dve.wait_ge(ln_ready.sem, v)
                                        nc.vector.tensor_tensor(delta[:, other, part], delta[:, other, part],
                                                                dx[:, other, part],
                                                                ALU.add).then_inc(delta_ready.sem, 1)
                            if "mix" in jobs_now:
                                for p in range(PAIRS):
                                    if s == 3 * p + 2:
                                        if v := due(dve, thg_ready, t, p + 1):
                                            dve.wait_ge(thg_ready.sem, v)
                                        if v := due(dve, ys_ready, t, p - 1):
                                            dve.wait_ge(ys_ready.sem, v)
                                        if v := due(dve, out_stored, t - 1, 1):
                                            dve.wait_ge(out_stored.sem, v)
                                        nc.vector.scalar_tensor_tensor(
                                            out=gate[:, p % 2].rearrange("p e t -> p (e t)"),
                                            in0=thg[:, p % 2].rearrange("p e t -> p (e t)"), scalar=1.0,
                                            in1=work[3][:], op0=ALU.add,
                                            op1=ALU.mult).then_inc(gate_ready.sem, 1)
                                    if s == 3 * p + 3:
                                        if v := due(dve, y_turned, t, p + 1):
                                            dve.wait_ge(y_turned.sem, v)
                                        if v := due(dve, gate_ready, t, p + 1):
                                            dve.wait_ge(gate_ready.sem, v)
                                        if v := due(dve, out_done, t - 1, TB):
                                            dve.wait_ge(out_done.sem, v)
                                        nc.vector.tensor_tensor(
                                            ys[:, 2 * p:2 * p + 2, :].rearrange("p e t -> p (e t)"), work[0][:],
                                            gate[:, p % 2].rearrange("p e t -> p (e t)"),
                                            ALU.mult).then_inc(ys_ready.sem, 1)
                                if s in (21, 30):
                                    b = (s - 21) // 9
                                    if v := due(dve, out_done, t, b + 1):
                                        dve.wait_ge(out_done.sem, v)
                                    if v := due(dve, z0_ready, t, TB):
                                        dve.wait_ge(z0_ready.sem, v)
                                    nc.vector.tensor_tensor(z[:, b], work[0][:], z[:, b],
                                                            ALU.add).then_inc(z_ready.sem, 1)
                            if "route" in jobs_now:
                                if s == 0:
                                    if v := due(dve, z_ready, t - 1, TB):
                                        dve.wait_ge(z_ready.sem, v)
                                    moments(z, mvz, "varz", var_z)
                                if s == 2:
                                    if v := due(dve, rz_ready, t, 1):
                                        dve.wait_ge(rz_ready.sem, v)
                                    minus_mean_times(small["nz"][:], mvz, small["rz"][:]).then_inc(nz_ready.sem, 1)
                                if s == 6:
                                    if v := due(dve, x1_ready, t, 1):
                                        dve.wait_ge(x1_ready.sem, v)
                                    moments(x1, mvh, "varh", var_h)
                                if s == 8:
                                    if v := due(dve, rh_ready, t, 1):
                                        dve.wait_ge(rh_ready.sem, v)
                                    minus_mean_times(small["nh"][:], mvh, small["rh"][:]).then_inc(nh_ready.sem, 1)
                                if s == 17:
                                    if v := due(dve, logits_done, t, 1):
                                        dve.wait_ge(logits_done.sem, v)
                                    link(nc.vector.tensor_reduce(
                                        small["nmx"][:],
                                        work[3][:, 0:TB * EXPERTS].rearrange("p (b e) -> p b e", b=TB),
                                        axis=AX.X, op=ALU.max))
                                    nc.vector.tensor_scalar(small["nmx"][:], small["nmx"][:], -1.0, None,
                                                            ALU.mult).then_inc(nmx_ready.sem, 1)
                                if s == 19:
                                    if v := due(dve, e_ready, t, TB):
                                        dve.wait_ge(e_ready.sem, v)
                                    for b in range(TB):
                                        last = nc.vector.max(top8[:, b], ex[:, b])
                                    link(last)
                                    for b in range(TB):
                                        nc.vector.match_replace(out=rem[:, b], in_to_replace=top8[:, b],
                                                                in_values=ex[:, b], imm_value=0.0)
                                    nc.vector.tensor_reduce(small["ts"][:], top8[:], axis=AX.X, op=ALU.add)
                                    link(nc.vector.reciprocal(small["rs"][:], small["se"][:]))
                                    nc.vector.tensor_tensor(small["ts"][:], small["ts"][:], small["rs"][:], ALU.mult)
                                    link(nc.vector.tensor_tensor(rem[:], ex[:], rem[:], ALU.subtract))
                                    nc.vector.tensor_tensor(ex[:], rem[:],
                                                            small["rs"][:].unsqueeze(2)
                                                            .to_broadcast([P, TB, EXPERTS]),
                                                            ALU.mult).then_inc(w_ready.sem, 1)
                                if s in (23, 25):
                                    b = (s - 23) // 2
                                    if v := due(dve, eb_done, t, b + 1):
                                        dve.wait_ge(eb_done.sem, v)
                                    if v := due(dve, w_ready, t, 1):
                                        dve.wait_ge(w_ready.sem, v)
                                    if v := due(dve, ys_ready, t, PAIRS):
                                        dve.wait_ge(ys_ready.sem, v)
                                    if v := due(dve, out_stored, t - 1, 1):
                                        dve.wait_ge(out_stored.sem, v)
                                    nc.vector.scalar_tensor_tensor(out=o[:, b], in0=h2[:, b],
                                                                   scalar=small["ts"][:, b:b + 1], in1=work[3][:],
                                                                   op0=ALU.mult,
                                                                   op1=ALU.add).then_inc(o_ready.sem, 1)
                                if s == 25:
                                    if v := due(dve, o_ready, t, TB):
                                        dve.wait_ge(o_ready.sem, v)
                                    moments(o, mvo, "varo", var_o)
                                if s == 27:
                                    if v := due(dve, ro_ready, t, 1):
                                        dve.wait_ge(ro_ready.sem, v)
                                    minus_mean_times(small["no"][:], mvo, small["ro"][:]).then_inc(no_ready.sem, 1)
                    if unfinished:
                        finish(*unfinished)

                @block.tensor
                def _(pe):
                    matmul, transpose = nc.tensor.matmul, nc.tensor.transpose
                    for t, jobs_now in enumerate(jobs):
                        now, other = (parity + t) % 2, (parity + t + 1) % 2
                        for s in range(SLOTS):
                            if "scan" in jobs_now:
                                if v := due(pe, scan_done, t, BANKS * (s + 1)):
                                    pe.wait_ge(scan_done.sem, v)
                                for b in range(TB):
                                    if v := due(pe, y_added, t, TB * (s - 1) + b + 1):
                                        pe.wait_ge(y_added.sem, v)
                                    for q in range(HALF):
                                        last = transpose(ht[:, b, q * P:(q + 1) * P],
                                                         h[:, s % 2, q, b * P:(b + 1) * P], ident[:])
                                    last.then_inc(ht_ready.sem, 1)
                            if "route" in jobs_now:
                                if s in (12, 14):
                                    b = (s - 12) // 2
                                    if v := due(pe, h2_ready, t, b + 1):
                                        pe.wait_ge(h2_ready.sem, v)
                                    if v := due(pe, gate_ready, t, PAIRS):
                                        pe.wait_ge(gate_ready.sem, v)
                                    if b and (v := due(pe, h2t_ready, t, b)):
                                        pe.wait_ge(h2t_ready.sem, v)
                                    if v := due(pe, o_ready, t - 1, TB):
                                        pe.wait_ge(o_ready.sem, v)
                                    for k in range(KD):
                                        last = transpose(work[3][:, k * P:(k + 1) * P],
                                                         h2[:, b, k * P:(k + 1) * P], ident[:])
                                    last.then_inc(h2_turned.sem, 1)
                                if s == 16:
                                    if v := due(pe, h2t_ready, t, TB):
                                        pe.wait_ge(h2t_ready.sem, v)
                                    for b in range(TB):
                                        logits = work[3][:, b * EXPERTS:(b + 1) * EXPERTS]
                                        for k in range(KD):
                                            matmul(logits, h2t[:, b, k, :], wrouter[:, k, :], start=(k == 0),
                                                   stop=False)
                                        last = matmul(logits, ones[:], rbias[:], start=False, stop=True)
                                    last.then_inc(logits_done.sem, 1)
                                if s == 20:
                                    if v := due(pe, w_ready, t, 1):
                                        pe.wait_ge(w_ready.sem, v)
                                    for b in range(TB):
                                        last = transpose(work[3][0:EXPERTS, b * P:(b + 1) * P], ex[:, b], ident[:])
                                    last.then_inc(w_turned.sem, 1)
                                if s in (22, 24):
                                    b = (s - 22) // 2
                                    if v := due(pe, wt_ready, t, 1):
                                        pe.wait_ge(wt_ready.sem, v)
                                    if b and (v := due(pe, o_ready, t, b)):
                                        pe.wait_ge(o_ready.sem, v)
                                    matmul(work[3][:], wt[:, b], ebias[:], start=True,
                                           stop=True).then_inc(eb_done.sem, 1)
                            if "scan" in jobs_now and s in (29, 31):
                                k0 = s - 29
                                if v := due(pe, xt_normed, t, TB):
                                    pe.wait_ge(xt_normed.sem, v)
                                if v := due(pe, o_ready, t, TB):
                                    pe.wait_ge(o_ready.sem, v)
                                if v := due(pe, gate_ready, t, PAIRS):
                                    pe.wait_ge(gate_ready.sem, v)
                                if v := due(pe, gate_rnt_ready, t, k0 // 2):
                                    pe.wait_ge(gate_rnt_ready.sem, v)
                                for k in range(2):
                                    for b in range(TB):
                                        last = transpose(work[3][:, k * T + b * P:k * T + (b + 1) * P],
                                                         h2[:, b, (k0 + k) * P:(k0 + k + 1) * P], ident[:])
                                last.then_inc(xt_turned.sem, 1)
                            if "norm" in jobs_now and s in (28, 29):
                                k0 = 2 * (s - 28)
                                if v := due(pe, rn_ready, t, TB):
                                    pe.wait_ge(rn_ready.sem, v)
                                if v := due(pe, acc_init, t, 3 + k0 // 2):
                                    pe.wait_ge(acc_init.sem, v)
                                if v := due(pe, rnt_ready, t - 1, 2):
                                    pe.wait_ge(rnt_ready.sem, v)
                                for k in range(2):
                                    for b in range(TB):
                                        last = transpose(pair_bank(k0 // 2)[:, k * T + b * P:k * T + (b + 1) * P],
                                                         xn[:, b, (k0 + k) * P:(k0 + k + 1) * P], ident[:])
                                last.then_inc(rn_turned.sem, 1)
                            if "prep" in jobs_now:
                                for p in range(PAIRS):
                                    if s in (3 * p + 1, 3 * p + 2):
                                        e = s - 3 * p - 1
                                        if v := due(pe, rnt_ready, t - 1, 2):
                                            pe.wait_ge(rnt_ready.sem, v)
                                        if v := due(pe, xin_ready, t, p - 1):
                                            pe.wait_ge(xin_ready.sem, v)
                                        for k in range(KD):
                                            last = matmul(pair_bank(p)[:, e * T:(e + 1) * T],
                                                          win[:, k, (2 * p + e) * P:(2 * p + e + 1) * P],
                                                          rnt[:, k, :], start=(k == 0), stop=(k == KD - 1))
                                        if e == 1:
                                            last.then_inc(in_done.sem, 1)
                                    if s == (12, 13, 14, 16)[p]:
                                        if v := due(pe, x_ready, t, p + 1):
                                            pe.wait_ge(x_ready.sem, v)
                                        if v := due(pe, xin_ready, t, 3):
                                            pe.wait_ge(xin_ready.sem, v)
                                        for et in (2 * p, 2 * p + 1):
                                            last = matmul(work[1][:, 0:T], wd1[:, et, :], x[:, et, :],
                                                          start=(et == 0), stop=(et == ET - 1))
                                        if p == PAIRS - 1:
                                            last.then_inc(low_done.sem, 1)
                                    if s == 13 + p:
                                        if v := due(pe, x_ready, t, p + 1):
                                            pe.wait_ge(x_ready.sem, v)
                                        if v := due(pe, xin_ready, t, 4):
                                            pe.wait_ge(xin_ready.sem, v)
                                        for et in (2 * p, 2 * p + 1):
                                            last = matmul(work[2][0:N, 0:T], wb[:, et, :], x[:, et, :],
                                                          start=(et == 0), stop=(et == ET - 1))
                                    if s == 18 + p:
                                        if v := due(pe, low_ready, t, 1):
                                            pe.wait_ge(low_ready.sem, v)
                                        if p % 2 and (v := due(pe, c_ready, t, 1)):
                                            pe.wait_ge(c_ready.sem, v)
                                        if v := due(pe, z_read, t, p - 1):
                                            pe.wait_ge(z_read.sem, v)
                                        for e in range(2):
                                            et = 2 * p + e
                                            last = matmul(pair_bank(p)[:, e * T:(e + 1) * T],
                                                          wd2[:, et * P:(et + 1) * P], low[:], start=True, stop=True)
                                        last.then_inc(z_done.sem, 1)
                                    if s == (22, 23, 26, 27)[p]:
                                        bank = pair_bank(p)
                                        if v := due(pe, xd_ready, t, p + 1):
                                            pe.wait_ge(xd_ready.sem, v)
                                        if v := due(pe, z_read, t, min(3 + p, PAIRS)):
                                            pe.wait_ge(z_read.sem, v)
                                        if v := due(pe, acc_init, t, p - 1):
                                            pe.wait_ge(acc_init.sem, v)
                                        for b in range(TB):
                                            for e in range(2):
                                                last = transpose(bank[:, (2 * b + e) * P:(2 * b + e + 1) * P],
                                                                 hv[:, p % 2, e, b * P:(b + 1) * P], ident[:])
                                        last.then_inc(xd_turned.sem, 1)
                                if s == 17:
                                    for b in range(TB):
                                        for et in range(ET):
                                            last = matmul(work[2][:, T + b * N:T + (b + 1) * N],
                                                          x[:, et, b * P:(b + 1) * P], wc[:, et, :],
                                                          start=(et == 0), stop=(et == ET - 1))
                                    last.then_inc(c_done.sem, 1)
                            if "mix" in jobs_now:
                                for p in range(PAIRS):
                                    if s == 3 * p:
                                        if v := due(pe, gate_rnt_ready, t - 1, 2):
                                            pe.wait_ge(gate_rnt_ready.sem, v)
                                        if v := due(pe, gate_ready, t, p):
                                            pe.wait_ge(gate_ready.sem, v)
                                        for e in range(2):
                                            for k in range(KD):
                                                last = matmul(work[3][:, e * T:(e + 1) * T],
                                                              wskip[:, k, (2 * p + e) * P:(2 * p + e + 1) * P],
                                                              rnt_gate[:, k, :], start=(k == 0), stop=(k == KD - 1))
                                        last.then_inc(skip_done.sem, 1)
                                    if s == 3 * p + 2:
                                        if v := due(pe, y_added, t - 1, SLOTS * TB):
                                            pe.wait_ge(y_added.sem, v)
                                        if v := due(pe, z_ready, t - 1, TB):
                                            pe.wait_ge(z_ready.sem, v)
                                        if p and (v := due(pe, ys_ready, t, p)):
                                            pe.wait_ge(ys_ready.sem, v)
                                        for e in range(2):
                                            for b in range(TB):
                                                last = transpose(work[0][:, (2 * e + b) * P:(2 * e + b + 1) * P],
                                                                 acc[:, other, b, (2 * p + e) * P:(2 * p + e + 1) * P],
                                                                 ident[:])
                                        last.then_inc(y_turned.sem, 1)
                                if 13 <= s < 13 + ET or 22 <= s < 22 + ET:
                                    b = int(s >= 22)
                                    et = s - (13, 22)[b]
                                    if v := due(pe, ys_ready, t, PAIRS):
                                        pe.wait_ge(ys_ready.sem, v)
                                    if b and (v := due(pe, z_ready, t, b)):
                                        pe.wait_ge(z_ready.sem, v)
                                    last = matmul(work[0][:], ys[:, et, b * P:(b + 1) * P], wout[:, et, :],
                                                  start=(et == 0), stop=(et == ET - 1))
                                    if et == ET - 1:
                                        last.then_inc(out_done.sem, 1)
            clear_semaphores()

        everything = ("norm", "prep", "scan", "mix", "route")
        section(-2, [("norm",), ("norm", "prep"), ("norm", "prep", "scan"), ("norm", "prep", "scan", "mix")], 0)
        with nc.Fori(0, (CHUNKS - 4) // 4) as quad:
            section(quad * 4 + 2, [everything] * 4, 0)
        section(CHUNKS - 2, [("prep", "scan", "mix", "route"), ("scan", "mix", "route"), ("mix", "route"), ("route",)], 0)


_INS = ['L0_attn_resid', 'L0_attn_norm_w', 'L0_attn_W_skip', 'L0_attn_W_in', 'L0_attn_conv_w', 'L0_attn_conv_b',
        'L0_attn_W_delta_1', 'L0_attn_W_delta_2', 'L0_attn_b_delta_2', 'L0_attn_W_B', 'L0_attn_W_C', 'L0_attn_A_log',
        'L0_attn_W_D', 'L0_attn_W_out', 'L0_ffn_router_weight', 'L0_ffn_router_bias', 'L0_ffn_expert_bias']


def kernel(**inputs):
    import numpy as _np
    import concourse.bacc as _bacc
    from concourse import mybir as _mybir
    from concourse.bass_utils import run_bass_kernel_spmd as _run

    nc = _bacc.Bacc("TRN2", target_bir_lowering=False, num_devices=1)
    arrays, args = {}, []
    for name in _INS:
        a = _np.ascontiguousarray(inputs[name])
        arrays[f"in_{name}"] = a
        args.append(nc.dram_tensor(f"in_{name}", a.shape, _mybir.dt.from_np(a.dtype), kind="ExternalInput").ap())
    shape = arrays["in_L0_attn_resid"].shape
    args.append(nc.dram_tensor("out_0", shape, _mybir.dt.float32, kind="ExternalOutput").ap())
    build(nc, *args)
    r = _run(nc, [arrays], core_ids=[0])
    return r.results[0]["out_0"]
```
